# Optimizing a Trainium2 kernel written in Bass

```python
import numpy as np
import jax
import jax.numpy as jnp

def _softmax(x, axis=-1):
    return jax.nn.softmax(x, axis=axis)

def _gelu(x):
    return jax.nn.gelu(x, approximate=True)

def _silu(x):
    return jax.nn.silu(x)

def _sigmoid(x):
    return jax.nn.sigmoid(x)

def _layernorm(x, axis=-1, eps=1e-05):
    m = jnp.mean(x, axis=axis, keepdims=True)
    v = jnp.var(x, axis=axis, keepdims=True)
    return (x - m) / jnp.sqrt(v + eps)

def _scatter_add(tgt, idx, src, axis=0):
    return tgt.at[idx].add(src)

def _segment_sum(src, seg, n):
    return jax.ops.segment_sum(src, seg, n)
kernel_name = 'mk_sandwich_d1_jaxref_r4_630815'

def setup_inputs(seed: int=0):
    np.random.seed(seed)
    _w = jnp.asarray

    def _L0_attn_setup():
        import jax, jax.numpy as jnp
        import numpy as np
        NUM_HEADS = 16
        WINDOW = 64
        key = jax.random.key(seed)
        k1, k2, k3 = jax.random.split(key, 3)
        B, T, C = (4, 1024, 256)
        x = jax.random.normal(k1, (B, T, C), dtype=jnp.float32)
        w_attn = jax.random.normal(k2, (3 * C, C), dtype=jnp.float32) * C ** (-0.5)
        w_proj = jax.random.normal(k3, (C, C), dtype=jnp.float32) * C ** (-0.5)
        return {'x': x, 'w_attn': w_attn, 'w_proj': w_proj}
    _L0_attn_in = _L0_attn_setup()

    def _L0_ffn_setup():
        import jax, jax.numpy as jnp
        import numpy as np
        DIM = 256
        HIDDEN = 768
        SCALE = 1.0 / 127.0

        def _dequant(w_int, dtype):
            return w_int.astype(dtype) * jnp.asarray(SCALE, dtype)
        key = jax.random.key(seed)
        k_x, k_g, k_u, k_d = jax.random.split(key, 4)
        x = jax.random.normal(k_x, (4, 512, DIM), dtype=jnp.float32)
        w_gate = jax.random.randint(k_g, (HIDDEN, DIM), -127, 128, dtype=jnp.int32)
        w_up = jax.random.randint(k_u, (HIDDEN, DIM), -127, 128, dtype=jnp.int32)
        w_down = jax.random.randint(k_d, (DIM, HIDDEN), -127, 128, dtype=jnp.int32)
        return {'x': x, 'w_gate': w_gate, 'w_up': w_up, 'w_down': w_down}
    _L0_ffn_in = _L0_ffn_setup()
    _d = {'L0_attn_x': _L0_attn_in['x'], 'L0_attn_w_attn': _L0_attn_in['w_attn'], 'L0_attn_w_proj': _L0_attn_in['w_proj'], 'L0_ffn_w_gate': _L0_ffn_in['w_gate'], 'L0_ffn_w_up': _L0_ffn_in['w_up'], 'L0_ffn_w_down': _L0_ffn_in['w_down']}
    _x0 = _d['L0_attn_x']
    _d['L0_attn_x'] = jax.random.normal(jax.random.fold_in(jax.random.key(seed), 1), (16, 1024, 256), dtype=_x0.dtype)
    del _x0
    return _d

def reference(L0_attn_x, L0_attn_w_attn, L0_attn_w_proj, L0_ffn_w_gate, L0_ffn_w_up, L0_ffn_w_down):

    def _L0_attn_ref(x, w_attn, w_proj):
        import jax, jax.numpy as jnp
        import numpy as np
        NUM_HEADS = 16
        WINDOW = 64
        B, T, C = x.shape
        H, W = (NUM_HEADS, WINDOW)
        D = C // H
        nW = T // W
        qkv = jnp.einsum('btc,ec->bte', x, w_attn)
        qkv = qkv.reshape(B, nW, W, 3, H, D)
        q, k, v = (qkv[:, :, :, 0], qkv[:, :, :, 1], qkv[:, :, :, 2])
        scale = 1.0 / jnp.sqrt(jnp.float32(D))
        att = jnp.einsum('bnihd,bnjhd->bnhij', q, k) * scale
        att = jax.nn.softmax(att, axis=-1)
        y = jnp.einsum('bnhij,bnjhd->bnihd', att, v)
        y = y.reshape(B, T, C)
        return jnp.einsum('btc,oc->bto', y, w_proj)

    def _L0_ffn_ref(x, w_gate, w_up, w_down):
        import jax, jax.numpy as jnp
        import numpy as np
        DIM = 256
        HIDDEN = 768
        SCALE = 1.0 / 127.0

        def _dequant(w_int, dtype):
            return w_int.astype(dtype) * jnp.asarray(SCALE, dtype)
        wg = _dequant(w_gate, x.dtype)
        wu = _dequant(w_up, x.dtype)
        wd = _dequant(w_down, x.dtype)
        gate = jnp.einsum('bsd,hd->bsh', x, wg)
        up = jnp.einsum('bsd,hd->bsh', x, wu)
        h = jax.nn.silu(gate) * up
        return jnp.einsum('bsh,dh->bsd', h, wd)
    x = L0_attn_x
    x = x + _layernorm(_L0_attn_ref(_layernorm(x, axis=-1), L0_attn_w_attn, L0_attn_w_proj), axis=-1)
    x = x + _layernorm(_L0_ffn_ref(_layernorm(x, axis=-1), L0_ffn_w_gate, L0_ffn_w_up, L0_ffn_w_down), axis=-1)
    return x

_drawn_inputs = setup_inputs


def setup_inputs(seed=0):
    import zlib

    import numpy as np

    out = dict(_drawn_inputs(seed))
    spreads = {}
    factors = {}
    for name, (base, spread) in spreads.items():
        noise = np.random.default_rng([zlib.crc32(name.encode()), seed]).standard_normal(out[name].shape)
        drawn = base * np.exp(spread * noise) if base else spread * noise
        out[name] = jnp.asarray(drawn.astype(out[name].dtype))
    for name, factor in factors.items():
        out[name] = (out[name] * factor).astype(out[name].dtype)
    return out
```

```python
import concourse.bass as bass
from concourse import mybir
from contextlib import ExitStack


def sandwich_block(nc, x_in, w_attn, w_proj, w_gate, w_up, w_down, out):
    f32, f32r, i32 = mybir.dt.float32, mybir.dt.float32r, mybir.dt.int32
    ALU = mybir.AluOpType
    ACT = mybir.ActivationFunctionType
    AX = mybir.AxisListType

    B, T, C = x_in.shape
    P = 128
    HEADS, WIN = 16, 64
    D = C // HEADS
    CB = C // P
    TT = 2
    GT = TT * P
    NG = B * T // GT
    HID = w_gate.shape[0]
    HB = HID // P
    HP = HB // 2
    PAIRS = HEADS // 2
    VW = 2 * (D + 1)
    LN_EPS = 1e-5
    Q_SCALE = D ** -0.5
    INT_SCALE = 1.0 / 127.0
    H_SCALE = 0.5 * INT_SCALE ** 3

    x_v = x_in.rearrange("b t c -> (b t) c").rearrange("(g t p) c -> g p t c", t=TT, p=P)
    out_v = out.rearrange("b t c -> (b t) c").rearrange("(g t p) c -> g p t c", t=TT, p=P)

    ctx = ExitStack()
    with ctx:
        def sb(name, shape, dt=f32):
            return ctx.enter_context(nc.sbuf_tensor(name, shape, dt))

        def pb(name, shape):
            return ctx.enter_context(nc.psum_tensor(name, shape, f32))

        def sem(name):
            return ctx.enter_context(nc.semaphore(name))

        wa_hi, wa_lo = sb("wa_hi", [P, CB, 3 * C], f32r), sb("wa_lo", [P, CB, 3 * C], f32r)
        wp_hi, wp_lo = sb("wp_hi", [P, CB, C], f32r), sb("wp_lo", [P, CB, C], f32r)
        wg_hi, wg_lo = sb("wg_hi", [P, CB, HID], f32r), sb("wg_lo", [P, CB, HID], f32r)
        wu_hi, wu_lo = sb("wu_hi", [P, CB, HID], f32r), sb("wu_lo", [P, CB, HID], f32r)
        wd_hi, wd_lo = sb("wd_hi", [P, HB, C], f32r), sb("wd_lo", [P, HB, C], f32r)
        wa_raw, wp_raw = sb("wa_raw", [P, 3 * CB, C]), sb("wp_raw", [P, CB, C])
        wg_int, wu_int = sb("wg_int", [P, HB, C], i32), sb("wu_int", [P, HB, C], i32)
        wd_int = sb("wd_int", [P, CB, HID], i32)
        wg_raw, wu_raw, wd_raw = sb("wg_raw", [P, HB, C]), sb("wu_raw", [P, HB, C]), sb("wd_raw", [P, CB, HID])
        ident = sb("ident", [P, P])
        even_head, odd_head = sb("even_head", [P, 1]), sb("odd_head", [P, 1])
        minus_half = sb("minus_half", [P, TT])

        x_sb = [sb(f"x_sb{i}", [P, TT, C]) for i in range(2)]
        x_res = [sb(f"x_res{i}", [P, TT, C]) for i in range(2)]
        x2 = [sb(f"x2_{i}", [P, TT, C]) for i in range(2)]
        out_sb = [sb(f"out_sb{i}", [P, TT, C]) for i in range(2)]
        xn, x2n = sb("xn", [P, TT, C]), sb("x2n", [P, TT, C])
        xT_hi, xT_lo = sb("xT_hi", [P, CB, GT + WIN], f32r), sb("xT_lo", [P, CB, GT + WIN], f32r)
        x2T_hi, x2T_lo = sb("x2T_hi", [P, CB, GT], f32r), sb("x2T_lo", [P, CB, GT], f32r)
        yT_hi, yT_lo = sb("yT_hi", [P, CB, GT], f32r), sb("yT_lo", [P, CB, GT], f32r)
        qT = sb("qT", [P, CB, GT])
        kT = sb("kT", [P, CB, 2, GT])
        v_sb = sb("v_sb", [P, 2 * TT, PAIRS, VW])
        probs = [sb(f"probs{t}", [P, HEADS * WIN]) for t in range(TT)]
        score_max = [sb(f"score_max{t}", [P, HEADS]) for t in range(TT)]
        pT = sb("pT", [P, 2 * TT, 4, P])
        inv_sum = sb("inv_sum", [P, HEADS])
        y_sb = sb("y_sb", [P, TT, C])
        attn_sb, ffn_sb = sb("attn_sb", [P, TT, C]), sb("ffn_sb", [P, TT, C])
        tanh_sb, gated, h_sb = (sb(n, [P, HP, 2 * GT]) for n in ("tanh_sb", "gated", "h_sb"))
        hT_hi, hT_lo = sb("hT_hi", [P, HP, 2, GT], f32r), sb("hT_lo", [P, HP, 2, GT], f32r)
        NORMS = ("in", "attn", "mid", "ffn")
        stats = {n: sb(f"stats_{n}", [P, TT, 6]) for n in NORMS}
        mean_var = {n: sb(f"mean_var_{n}", [P, TT, 2]) for n in NORMS}
        var_eps = {n: sb(f"var_eps_{n}", [P, TT]) for n in NORMS}
        rstd = {n: sb(f"rstd_{n}", [P, TT]) for n in NORMS}
        neg_mr = {n: sb(f"neg_mr_{n}", [P, TT]) for n in NORMS}

        score_ps = pb("score_ps", [P, 4, 512])
        turn0, turn1 = pb("turn0", [P, 512]), pb("turn1", [P, 512])
        pT_ps, y_ps = pb("pT_ps", [P, 512]), pb("y_ps", [P, 512])

        w_loaded = [sem(f"w_loaded{i}") for i in range(5)]
        ident_set, masks_set, ones_set = sem("ident_set"), sem("masks_set"), sem("ones_set")
        w_cast = sem("w_cast")
        wT_done, wT_hi_done, wT_lo_done = sem("wT_done"), sem("wT_hi_done"), sem("wT_lo_done")
        x_loaded = [sem(f"x_loaded{i}") for i in range(2)]
        x_kept = [sem(f"x_kept{i}") for i in range(2)]
        stored = [sem(f"stored{i}") for i in range(2)]
        norm_steps = {n: sem(f"norm_steps_{n}") for n in NORMS}
        rstd_done = {n: sem(f"rstd_done_{n}") for n in NORMS}
        normed = {n: sem(f"normed_{n}") for n in NORMS}
        xT_done, xT_hi_done, xT_lo_done = sem("xT_done"), sem("xT_hi_done"), sem("xT_lo_done")
        xT_wrapped = sem("xT_wrapped")
        yT_done, yT_hi_done, yT_lo_done = sem("yT_done"), sem("yT_hi_done"), sem("yT_lo_done")
        x2T_done, x2T_hi_done, x2T_lo_done = sem("x2T_done"), sem("x2T_hi_done"), sem("x2T_lo_done")
        q_done, k_done, v_done = sem("q_done"), sem("k_done"), sem("v_done")
        q_out, k_even_out, k_odd_out = sem("q_out"), sem("k_even_out"), sem("k_odd_out")
        v_even_out, v_odd_out = sem("v_even_out"), sem("v_odd_out")
        scores_done = sem("scores_done")
        softmax_steps = sem("softmax_steps")
        exp_done = sem("exp_done")
        pT_done, pT_out, pv_done = sem("pT_done"), sem("pT_out"), sem("pv_done")
        y_steps = sem("y_steps")
        proj_done, attn_out, x2_done = sem("proj_done"), sem("attn_out"), sem("x2_done")
        gate_done, up_done = sem("gate_done"), sem("up_done")
        tanh_done, glu_steps = sem("tanh_done"), sem("glu_steps")
        h_hi_done, h_lo_done = sem("h_hi_done"), sem("h_lo_done")
        down_done, ffn_out, out_done = sem("down_done"), sem("ffn_out"), sem("out_done")

        class Group:

            def __init__(self, k, c):
                self.k, self.c = k, c
                self.number, self.parity, self.half = 2 * k + c, c % 2, k + c // 2
                self.live = not isinstance(k, int) or 0 <= 2 * k + c < NG

            def shift(self, by):
                return Group(self.k, self.c + by)

        def count(g, each, k):
            return g.number * each + k

        def nth(g, k=1):
            return (g.half + k) * 16

        def ahead(eng, *values):
            for v in values:
                if not isinstance(v, int):
                    eng.compute_val(v)

        LOOP_FROM, LOOP_TO = 4, NG - 2
        assert NG % 2 == 0

        def steps(eng, step):
            for s in range(-1, LOOP_FROM):
                step(Group(0, s))
            with eng.Fori(LOOP_FROM // 2, LOOP_TO // 2) as k:
                step(Group(k, 0))
                step(Group(k, 1))
            for s in range(LOOP_TO, NG + 2):
                step(Group(0, s))

        block = ctx.enter_context(nc.Block())

        def weight_turns():
            turns = []
            for raw, hi, lo, n in ((wa_raw, wa_hi, wa_lo, 3 * CB), (wp_raw, wp_hi, wp_lo, CB),
                                   (wg_raw, wg_hi, wg_lo, HB), (wu_raw, wu_hi, wu_lo, HB)):
                for r in range(0, n, 2):
                    blocks = [raw[:, r + i, c * P:(c + 1) * P] for c in range(CB) for i in range(2)]
                    turns.append((raw, blocks, hi[:, :, r * P:(r + 2) * P], lo[:, :, r * P:(r + 2) * P]))
            for b in range(0, HB, 2):
                blocks = [wd_raw[:, r, (b + i) * P:(b + i + 1) * P] for i in range(2) for r in range(CB)]
                turns.append((wd_raw, blocks, wd_hi[:, b:b + 2, :], wd_lo[:, b:b + 2, :]))
            return turns

        TURNS = weight_turns()

        @block.sync
        def _(sp):
            def load(g):
                ahead(sp, g.number, nth(g, 0), count(g.shift(-2), 1, 1))
                if g.shift(-2).live:
                    sp.wait_ge(x_kept[g.parity], nth(g, 0))
                    sp.wait_ge(normed["in"], count(g.shift(-2), 1, 1))
                sp.dma_start(x_sb[g.parity][:, :, :], x_v[g.number, :, :, :]).then_inc(x_loaded[g.parity], 16)

            load(Group(0, 0))
            sp.dma_start(wa_raw[:, :, :], w_attn.rearrange("(r p) c -> p r c", p=P)).then_inc(w_loaded[0], 16)
            sp.dma_start(wp_raw[:, :, :], w_proj.rearrange("(r p) c -> p r c", p=P)).then_inc(w_loaded[1], 16)
            sp.dma_start(wg_int[:, :, :], w_gate.rearrange("(r p) c -> p r c", p=P)).then_inc(w_loaded[2], 16)
            sp.dma_start(wu_int[:, :, :], w_up.rearrange("(r p) c -> p r c", p=P)).then_inc(w_loaded[3], 16)
            sp.dma_start(wd_int[:, :, :], w_down.rearrange("(r p) c -> p r c", p=P)).then_inc(w_loaded[4], 16)

            def step(s):
                a, e = s.shift(1), s.shift(-2)
                if a.live:
                    ahead(sp, nth(a), count(a.shift(-2), 1, 1))
                    sp.wait_ge(x_loaded[a.parity], nth(a))
                    if a.shift(-2).live:
                        sp.wait_ge(x2_done, count(a.shift(-2), 1, 1))
                    sp.dma_start(x_res[a.parity][:, :, :], x_sb[a.parity][:, :, :])\
                      .then_inc(x_kept[a.parity], 16)
                if e.live:
                    ahead(sp, e.number, count(e, 1, 1))
                    sp.wait_ge(out_done, count(e, 1, 1))
                    sp.dma_start(out_v[e.number, :, :, :], out_sb[e.parity][:, :, :])\
                      .then_inc(stored[e.parity], 16)
                if a.shift(1).live:
                    load(a.shift(1))

            steps(sp, step)
            for i in range(2):
                sp.wait_ge(stored[i], NG // 2 * 16)

        @block.gpsimd
        def _(pool):
            pool.memset(ident[:, :], 0.0).then_inc(ident_set, 1)
            pool.memset(minus_half[:, :], -0.5).then_inc(ones_set, 1)
            pool.wait_ge(ident_set, 1)
            pool.affine_select(out=ident[:, :], in_=ident[:, :], compare_op=ALU.not_equal, fill=1.0,
                               base=0, pattern=[[-1, P]], channel_multiplier=1).then_inc(ident_set, 1)
            pool.memset(v_sb[:, :, :, :], 0.0).then_inc(ones_set, 1)
            pool.wait_ge(ones_set, 2)
            pool.memset(v_sb[0:WIN, :, :, D:D + 1], 1.0).then_inc(ones_set, 1)
            pool.memset(v_sb[WIN:P, :, :, VW - 1:VW], 1.0).then_inc(ones_set, 1)
            pool.wait_ge(ones_set, 4)

            def rstd_of(norm, g):
                pool.wait_ge(norm_steps[norm], count(g, 4, 3))
                if g.shift(-1).live:
                    pool.wait_ge(normed[norm], count(g.shift(-1), 1, 1))
                pool.tensor_tensor(rstd[norm][:, :], var_eps[norm][:, :], minus_half[:, :], ALU.pow)\
                    .then_inc(rstd_done[norm], 1)

            def h_low(g, j):
                pool.wait_ge(h_hi_done, count(g, HP, j + 1))
                pool.tensor_tensor(hT_lo[:, j, :, :], h_sb[:, j, :].rearrange("p (b t) -> p b t", b=2),
                                   hT_hi[:, j, :, :].bitcast(f32), ALU.subtract).then_inc(h_lo_done, 1)

            def wrap(g):
                ahead(pool, count(g, 1, 1))
                pool.wait_ge(ident_set, 2)
                pool.wait_ge(xT_lo_done, count(g, 1, 1))
                for x in (xT_hi, xT_lo):
                    pool.tensor_copy(x[:, :, GT:GT + WIN], x[:, :, 0:WIN].bitcast(f32)).then_inc(xT_wrapped, 1)

            def step(s):
                a, c, e = s.shift(1), s.shift(-1), s.shift(-2)
                if c.live:
                    rstd_of("attn", c)
                if a.live:
                    rstd_of("in", a)
                if c.live:
                    rstd_of("mid", c)
                if e.live:
                    rstd_of("ffn", e)
                if a.live:
                    wrap(a)
                if c.live:
                    for j in range(HP):
                        h_low(c, j)

            steps(pool, step)

        @block.tensor
        def _(pe):
            pe.wait_ge(ident_set, 2)
            for n, (raw, blocks, _, _) in enumerate(TURNS):
                if raw is wa_raw or raw is wp_raw:
                    pe.wait_ge(w_loaded[0 if raw is wa_raw else 1], 16)
                else:
                    pe.wait_ge(w_cast, [wg_raw, wu_raw, wd_raw].index(raw) + 1)
                if n >= 2:
                    pe.wait_ge(wT_lo_done, n - 1)
                bank = (turn0, turn1)[n % 2]
                for i, b in enumerate(blocks):
                    mm = pe.transpose(bank[:, i * P:(i + 1) * P], b, ident[:, :])
                mm.then_inc(wT_done, 1)
            pe.wait_ge(wT_lo_done, len(TURNS))
            pe.wait_ge(ones_set, 4)

            def turn_tokens(bank, src, done):
                for c in range(CB):
                    for t in range(TT):
                        mm = pe.transpose(bank[:, c * GT + t * P:c * GT + (t + 1) * P],
                                          src[:, t, c * P:(c + 1) * P], ident[:, :])
                mm.then_inc(done, 1)

            def split_product(out_ap, stationary, moving, blocks):
                n = len(blocks)
                for i, blk in enumerate(blocks):
                    (s_hi, s_lo), (m_hi, m_lo) = stationary(blk), moving(blk)
                    pe.matmul(out_ap, s_hi, m_hi, start=(i == 0), stop=False)
                    pe.matmul(out_ap, s_hi, m_lo, start=False, stop=False)
                    mm = pe.matmul(out_ap, s_lo, m_hi, start=False, stop=(i == n - 1))
                return mm

            def q_or_k(bank, first_block, done):
                for m in range(CB):
                    col = (first_block + m) * P
                    mm = split_product(bank[:, m * GT:(m + 1) * GT],
                                       lambda c: (wa_hi[:, c, col:col + P], wa_lo[:, c, col:col + P]),
                                       lambda c: (xT_hi[:, c, 0:GT], xT_lo[:, c, 0:GT]), range(CB))
                mm.then_inc(done, 1)

            def values(bank, half):
                for i in range(2):
                    at = (2 * half + i) * WIN
                    mm = split_product(bank[:, i * C:(i + 1) * C],
                                       lambda c: (xT_hi[:, c, at:at + P], xT_lo[:, c, at:at + P]),
                                       lambda c: (wa_hi[:, c, 2 * C:3 * C], wa_lo[:, c, 2 * C:3 * C]),
                                       range(CB))
                mm.then_inc(v_done, 1)

            def scores(t):
                for m in range(CB):
                    for b in range(4):
                        for w in range(2):
                            at = t * P + w * WIN
                            mm = pe.matmul(score_ps[w * WIN:(w + 1) * WIN, b, m * P:(m + 1) * P],
                                           qT[32 * b:32 * b + 32, m, at:at + WIN],
                                           kT[32 * b:32 * b + 32, m, :, at:at + WIN],
                                           start=True, stop=True)
                mm.then_inc(scores_done, 1)

            def turn_probs(g, t, m):
                unit = 2 * t + m
                if m == 0:
                    pe.wait_ge(exp_done, count(g, TT, t + 1))
                if unit or g.shift(-1).live:
                    pe.wait_ge(pT_out, count(g, 4, unit))
                for b in range(4):
                    at = (2 * b + m) * P
                    mm = pe.transpose(pT_ps[:, b * P:(b + 1) * P], probs[t][:, at:at + P], ident[:, :])
                mm.then_inc(pT_done, 1)

            def weigh_values(g, t, m):
                unit = 2 * t + m
                pe.wait_ge(pT_out, count(g, 4, unit + 1))
                if unit == 0:
                    pe.wait_ge(v_even_out, count(g, 2, 2))
                    pe.wait_ge(v_odd_out, count(g, 2, 2))
                if m == 0 and (t or g.shift(-1).live):
                    pe.wait_ge(y_steps, count(g, 4, 2 * t))
                for b in range(4):
                    pair = 4 * m + b
                    for w in range(2):
                        mm = pe.matmul(y_ps[w * WIN:(w + 1) * WIN, pair * VW:(pair + 1) * VW],
                                       pT[:, unit, b, w * WIN:(w + 1) * WIN],
                                       v_sb[:, 2 * t + w, pair, :], start=True, stop=True)
                mm.then_inc(pv_done, 1)

            def project():
                for t in range(TT):
                    mm = split_product(turn0[:, t * C:(t + 1) * C],
                                       lambda c: (yT_hi[:, c, t * P:(t + 1) * P], yT_lo[:, c, t * P:(t + 1) * P]),
                                       lambda c: (wp_hi[:, c, :], wp_lo[:, c, :]), range(CB))
                mm.then_inc(proj_done, 1)

            def hidden(bank, hi, lo, j, done):
                for i in range(2):
                    col = (2 * j + i) * P
                    mm = split_product(bank[:, i * GT:(i + 1) * GT],
                                       lambda c: (hi[:, c, col:col + P], lo[:, c, col:col + P]),
                                       lambda c: (x2T_hi[:, c, :], x2T_lo[:, c, :]), range(CB))
                mm.then_inc(done, 1)

            def down():
                for t in range(TT):
                    def h_of(x, k):
                        return x[:, k // 2, k % 2, t * P:(t + 1) * P]
                    mm = split_product(turn0[:, t * C:(t + 1) * C],
                                       lambda k: (h_of(hT_hi, k), h_of(hT_lo, k)),
                                       lambda k: (wd_hi[:, k, :], wd_lo[:, k, :]), range(HB))
                mm.then_inc(down_done, 1)

            def step(s):
                a, b, c, e = s.shift(1), s, s.shift(-1), s.shift(-2)
                if c.live:
                    pe.wait_ge(y_steps, count(c, 4, 4))
                    if e.live:
                        pe.wait_ge(glu_steps, count(e, 2 * HP, 5))
                    else:
                        pe.wait_ge(q_out, count(b, 1, 1))
                    turn_tokens(turn0, y_sb, yT_done)
                if b.live:
                    if e.live:
                        pe.wait_ge(glu_steps, count(e, 2 * HP, 6))
                    pe.wait_ge(k_even_out, count(b, 1, 1))
                    pe.wait_ge(k_odd_out, count(b, 1, 1))
                    pe.wait_ge(xT_wrapped, count(b, 2, 2))
                    values(turn1, 0)
                    pe.wait_ge(q_out, count(b, 1, 1))
                    if not e.live and c.live:
                        pe.wait_ge(softmax_steps, count(c, 4, 4))
                    scores(0)
                if c.live:
                    pe.wait_ge(yT_lo_done, count(c, 1, 1))
                    project()
                if b.live:
                    pe.wait_ge(v_even_out, count(b, 2, 1))
                    pe.wait_ge(v_odd_out, count(b, 2, 1))
                    values(turn1, 1)
                if e.live:
                    pe.wait_ge(h_lo_done, count(e, HP, HP))
                    if c.live:
                        pe.wait_ge(attn_out, count(c, 1, 1))
                    else:
                        pe.wait_ge(glu_steps, count(e, 2 * HP, 5))
                    down()
                if b.live:
                    turn_probs(b, 0, 0)
                    pe.wait_ge(softmax_steps, count(b, 4, 2))
                    scores(1)
                    turn_probs(b, 0, 1)
                    weigh_values(b, 0, 0)
                if a.live:
                    pe.wait_ge(normed["in"], count(a, 1, 1))
                    if b.live:
                        pe.wait_ge(v_even_out, count(b, 2, 2))
                        pe.wait_ge(v_odd_out, count(b, 2, 2))
                    turn_tokens(turn1, xn, xT_done)
                if b.live:
                    weigh_values(b, 0, 1)
                if a.live:
                    pe.wait_ge(xT_lo_done, count(a, 1, 1))
                    if e.live:
                        pe.wait_ge(ffn_out, count(e, 1, 1))
                    elif c.live:
                        pe.wait_ge(attn_out, count(c, 1, 1))
                    elif b.live:
                        pe.wait_ge(q_out, count(b, 1, 1))
                    q_or_k(turn0, 0, q_done)
                    q_or_k(turn1, CB, k_done)
                if c.live:
                    pe.wait_ge(normed["mid"], count(c, 1, 1))
                    if a.live:
                        pe.wait_ge(q_out, count(a, 1, 1))
                    elif e.live:
                        pe.wait_ge(ffn_out, count(e, 1, 1))
                    turn_tokens(turn0, x2n, x2T_done)
                if b.live:
                    turn_probs(b, 1, 0)
                if c.live:
                    pe.wait_ge(x2T_lo_done, count(c, 1, 1))
                    if b.live:
                        pe.wait_ge(softmax_steps, count(b, 4, 4))
                    else:
                        pe.wait_ge(glu_steps, count(e, 2 * HP, 4))
                    hidden(score_ps[:, 0, :], wg_hi, wg_lo, 0, gate_done)
                    hidden(score_ps[:, 1, :], wu_hi, wu_lo, 0, up_done)
                if b.live:
                    turn_probs(b, 1, 1)
                    weigh_values(b, 1, 0)
                if c.live:
                    hidden(score_ps[:, 2, :], wg_hi, wg_lo, 1, gate_done)
                    hidden(score_ps[:, 3, :], wu_hi, wu_lo, 1, up_done)
                if b.live:
                    weigh_values(b, 1, 1)
                if c.live:
                    hidden(turn0, wg_hi, wg_lo, 2, gate_done)
                    if a.live:
                        pe.wait_ge(k_even_out, count(a, 1, 1))
                        pe.wait_ge(k_odd_out, count(a, 1, 1))
                    elif b.live:
                        pe.wait_ge(v_even_out, count(b, 2, 2))
                        pe.wait_ge(v_odd_out, count(b, 2, 2))
                    else:
                        pe.wait_ge(glu_steps, count(e, 2 * HP, 6))
                    hidden(turn1, wu_hi, wu_lo, 2, up_done)

            steps(pe, step)

        @block.scalar
        def _(act):
            def split(x):
                return x.rearrange("p (a b) -> p a b", a=2)

            for n, (_, _, hi, _) in enumerate(TURNS):
                act.wait_ge(wT_done, n + 1)
                act.activation(hi, split((turn0, turn1)[n % 2][:, :]), ACT.Copy).then_inc(wT_hi_done, 1)
            act.wait_ge(masks_set, 2)

            def copy(to, of, done, scale=1.0):
                act.activation(to, of, ACT.Copy, scale=scale).then_inc(done, 1)

            def normalise(norm, g, to, of):
                act.wait_ge(norm_steps[norm], count(g, 4, 4))
                for t in range(TT):
                    last = act.activation(to[:, t, :], of[:, t, :], ACT.Identity,
                                          scale=rstd[norm][:, t:t + 1], bias=neg_mr[norm][:, t:t + 1])
                last.then_inc(normed[norm], 1)

            def even_values(g, t):
                act.wait_ge(v_done, count(g, 2, t + 1))
                copy(v_sb[0:WIN, 2 * t:2 * t + 2, :, 0:D],
                     turn1[0:WIN, :].rearrange("p (w h e d) -> p w h e d", w=2, e=2, d=D)[:, :, :, 0, :],
                     v_even_out)

            def exponentials(g, t):
                act.wait_ge(softmax_steps, count(g, 4, 2 * t + 2))
                act.activation(probs[t][:, :], probs[t][:, :], ACT.Exp).then_inc(exp_done, 1)

            def probs_out(g, unit):
                act.wait_ge(pT_done, count(g, 4, unit + 1))
                copy(pT[:, unit, :, :], pT_ps[:, :].rearrange("p (b i) -> p b i", b=4), pT_out)

            def tanh(g, j, bank):
                act.wait_ge(gate_done, count(g, HP, j + 1))
                act.activation(tanh_sb[:, j, :], bank, ACT.Tanh, scale=0.5 * INT_SCALE).then_inc(tanh_done, 1)

            def h_high(g, j):
                act.wait_ge(glu_steps, count(g, 2 * HP, 2 * j + 2))
                if j == 0 and g.shift(-1).live:
                    act.wait_ge(down_done, count(g.shift(-1), 1, 1))
                copy(hT_hi[:, j, :, :], split(h_sb[:, j, :]), h_hi_done)

            def step(s):
                a, b, c, e = s.shift(1), s, s.shift(-1), s.shift(-2)
                if c.live:
                    act.wait_ge(yT_done, count(c, 1, 1))
                    copy(yT_hi[:, :, :], split(turn0[:, :]), yT_hi_done)
                if b.live:
                    even_values(b, 0)
                if c.live:
                    act.wait_ge(proj_done, count(c, 1, 1))
                    if c.shift(-1).live:
                        act.wait_ge(x2_done, count(c.shift(-1), 1, 1))
                    copy(attn_sb[:, :, :], split(turn0[:, :]), attn_out)
                if b.live:
                    exponentials(b, 0)
                    even_values(b, 1)
                if c.live:
                    normalise("attn", c, attn_sb, attn_sb)
                if e.live:
                    act.wait_ge(down_done, count(e, 1, 1))
                    if e.shift(-1).live:
                        act.wait_ge(out_done, count(e.shift(-1), 1, 1))
                    copy(ffn_sb[:, :, :], split(turn0[:, :]), ffn_out)
                if b.live:
                    probs_out(b, 0)
                if a.live:
                    if b.live:
                        act.wait_ge(xT_done, count(b, 1, 1))
                    normalise("in", a, xn, x_sb[a.parity])
                if b.live:
                    probs_out(b, 1)
                    exponentials(b, 1)
                if c.live:
                    if c.shift(-1).live:
                        act.wait_ge(x2T_done, count(c.shift(-1), 1, 1))
                    normalise("mid", c, x2n, x2[c.parity])
                if a.live:
                    act.wait_ge(xT_done, count(a, 1, 1))
                    copy(xT_hi[:, :, 0:GT], split(turn1[:, :]), xT_hi_done)
                if e.live:
                    normalise("ffn", e, ffn_sb, ffn_sb)
                if a.live:
                    act.wait_ge(q_done, count(a, 1, 1))
                    copy(qT[:, :, :], split(turn0[:, :]), q_out, scale=Q_SCALE)
                    act.wait_ge(k_done, count(a, 1, 1))
                    copy(kT[:, :, 0, :], split(turn1[:, :]), k_even_out, scale=even_head[:, :])
                if c.live:
                    act.wait_ge(x2T_done, count(c, 1, 1))
                    copy(x2T_hi[:, :, :], split(turn0[:, :]), x2T_hi_done)
                if b.live:
                    probs_out(b, 2)
                if c.live:
                    tanh(c, 0, score_ps[:, 0, :])
                if b.live:
                    probs_out(b, 3)
                if c.live:
                    tanh(c, 1, score_ps[:, 2, :])
                    h_high(c, 0)
                    tanh(c, 2, turn0[:, :])
                    h_high(c, 1)
                    h_high(c, 2)

            steps(act, step)

        @block.vector
        def _(dve):
            def split(x):
                return x.rearrange("p (a b) -> p a b", a=2)

            dve.wait_ge(ident_set, 2)
            head_rows = ident[:, :].rearrange("p (a e d) -> p a e d", e=2, d=D)
            dve.tensor_reduce(even_head[:, :], head_rows[:, :, 0, :], AX.XY, ALU.add).then_inc(masks_set, 1)
            dve.tensor_reduce(odd_head[:, :], head_rows[:, :, 1, :], AX.XY, ALU.add).then_inc(masks_set, 1)
            for i, (to, of) in enumerate(((wg_raw, wg_int), (wu_raw, wu_int), (wd_raw, wd_int))):
                dve.wait_ge(w_loaded[2 + i], 16)
                dve.tensor_copy(to[:, :, :], of[:, :, :]).then_inc(w_cast, 1)
            for n, (_, _, hi, lo) in enumerate(TURNS):
                dve.wait_ge(wT_hi_done, n + 1)
                dve.tensor_tensor(lo, split((turn0, turn1)[n % 2][:, :]), hi.bitcast(f32),
                                  ALU.subtract).then_inc(wT_lo_done, 1)
            dve.wait_ge(masks_set, 2)
            dve.wait_ge(ones_set, 4)

            def low(to, bank, hi, done):
                dve.tensor_tensor(to, split(bank[:, :]), hi.bitcast(f32),
                                  ALU.subtract).then_inc(done, 1)

            def statistics(norm, g, x):
                for t in range(TT):
                    last = dve.bn_stats(stats[norm][:, t, :], x[:, t, :])
                last.then_inc(norm_steps[norm], 1)
                ahead(dve, count(g, 4, 1))
                dve.wait_ge(masks_set, 2)
                dve.wait_ge(norm_steps[norm], count(g, 4, 1))
                for t in range(TT):
                    last = dve.bn_aggr(mean_var[norm][:, t, :], stats[norm][:, t, :])
                last.then_inc(norm_steps[norm], 1)
                dve.wait_ge(norm_steps[norm], count(g, 4, 2))
                dve.tensor_scalar(var_eps[norm][:, :], mean_var[norm][:, :, 1], LN_EPS, None,
                                  ALU.add).then_inc(norm_steps[norm], 1)

            def shift_of(norm, g):
                dve.wait_ge(rstd_done[norm], count(g, 1, 1))
                dve.scalar_tensor_tensor(out=neg_mr[norm][:, :], in0=mean_var[norm][:, :, 0], scalar=-1.0,
                                         in1=rstd[norm][:, :], op0=ALU.mult, op1=ALU.mult)\
                   .then_inc(norm_steps[norm], 1)

            def odd_values(g, t):
                dve.wait_ge(v_done, count(g, 2, t + 1))
                windows = v_sb[WIN:P, 1:3, :, D + 1:VW - 1] if t == 0 else v_sb[WIN:P, 3::-3, :, D + 1:VW - 1]
                dve.tensor_copy(windows,
                                turn1[WIN:P, :].rearrange("p (w h e d) -> p w h e d", w=2, e=2, d=D)[:, :, :, 1, :])\
                   .then_inc(v_odd_out, 1)

            def softmax(g, t):
                dve.wait_ge(scores_done, count(g, TT, t + 1))
                dve.tensor_reduce(score_max[t][:, :].rearrange("p (b h) -> p b h", b=4),
                                  score_ps[:, :, 0:4 * WIN].rearrange("p b (h j) -> p b h j", j=WIN),
                                  AX.X, ALU.max).then_inc(softmax_steps, 1)
                dve.wait_ge(softmax_steps, count(g, 4, 2 * t + 1))
                dve.tensor_tensor(probs[t][:, :].rearrange("p (b h j) -> p b h j", b=4, j=WIN),
                                  score_ps[:, :, 0:4 * WIN].rearrange("p b (h j) -> p b h j", j=WIN),
                                  score_max[t][:, :].rearrange("p (b h) -> p b h", b=4).unsqueeze(3)
                                  .broadcast_to([P, 4, 4, WIN]), ALU.subtract).then_inc(softmax_steps, 1)

            def attention_out(g, t):
                y = y_ps[:, 0:HEADS * (D + 1)].rearrange("p (h d) -> p h d", d=D + 1)
                dve.wait_ge(pv_done, count(g, 4, 2 * t + 2))
                dve.reciprocal(inv_sum[:, :], y[:, :, D]).then_inc(y_steps, 1)
                dve.wait_ge(y_steps, count(g, 4, 2 * t + 1))
                dve.tensor_tensor(y_sb[:, t, :].rearrange("p (h d) -> p h d", d=D), y[:, :, 0:D],
                                  inv_sum[:, :].unsqueeze(2).broadcast_to([P, HEADS, D]),
                                  ALU.mult).then_inc(y_steps, 1)

            def gated_linear(g, j, g_bank, u_bank):
                dve.wait_ge(tanh_done, count(g, HP, j + 1))
                dve.scalar_tensor_tensor(out=gated[:, j, :], in0=tanh_sb[:, j, :], scalar=1.0, in1=g_bank,
                                         op0=ALU.add, op1=ALU.mult).then_inc(glu_steps, 1)
                dve.wait_ge(glu_steps, count(g, 2 * HP, 2 * j + 1))
                dve.wait_ge(up_done, count(g, HP, j + 1))
                if g.shift(-1).live:
                    dve.wait_ge(h_lo_done, count(g.shift(-1), HP, j + 1))
                dve.scalar_tensor_tensor(out=h_sb[:, j, :], in0=u_bank, scalar=H_SCALE, in1=gated[:, j, :],
                                         op0=ALU.mult, op1=ALU.mult).then_inc(glu_steps, 1)

            def step(s):
                a, b, c, e = s.shift(1), s, s.shift(-1), s.shift(-2)
                if c.live:
                    dve.wait_ge(yT_hi_done, count(c, 1, 1))
                    low(yT_lo[:, :, :], turn0, yT_hi[:, :, :], yT_lo_done)
                if b.live:
                    odd_values(b, 0)
                    softmax(b, 0)
                if c.live:
                    dve.wait_ge(attn_out, count(c, 1, 1))
                    statistics("attn", c, attn_sb)
                if b.live:
                    odd_values(b, 1)
                if a.live:
                    dve.wait_ge(x_loaded[a.parity], nth(a))
                    statistics("in", a, x_sb[a.parity])
                if c.live:
                    shift_of("attn", c)
                if a.live:
                    shift_of("in", a)
                if b.live:
                    softmax(b, 1)
                if c.live:
                    dve.wait_ge(normed["attn"], count(c, 1, 1))
                    dve.wait_ge(x_kept[c.parity], nth(c))
                    if c.shift(-2).live:
                        dve.wait_ge(out_done, count(c.shift(-2), 1, 1))
                    dve.tensor_tensor(x2[c.parity][:, :, :], attn_sb[:, :, :], x_res[c.parity][:, :, :],
                                      ALU.add).then_inc(x2_done, 1)
                    dve.wait_ge(x2_done, count(c, 1, 1))
                    statistics("mid", c, x2[c.parity])
                if e.live:
                    dve.wait_ge(ffn_out, count(e, 1, 1))
                    statistics("ffn", e, ffn_sb)
                if b.live:
                    attention_out(b, 0)
                if c.live:
                    shift_of("mid", c)
                if e.live:
                    shift_of("ffn", e)
                if a.live:
                    dve.wait_ge(xT_hi_done, count(a, 1, 1))
                    low(xT_lo[:, :, 0:GT], turn1, xT_hi[:, :, 0:GT], xT_lo_done)
                if e.live:
                    dve.wait_ge(normed["ffn"], count(e, 1, 1))
                    if e.shift(-2).live:
                        dve.wait_ge(stored[e.parity], nth(e, 0))
                    dve.tensor_tensor(out_sb[e.parity][:, :, :], ffn_sb[:, :, :], x2[e.parity][:, :, :],
                                      ALU.add).then_inc(out_done, 1)
                if a.live:
                    dve.wait_ge(k_even_out, count(a, 1, 1))
                    dve.tensor_scalar(kT[:, :, 1, :], split(turn1[:, :]), odd_head[:, :], None,
                                      ALU.mult).then_inc(k_odd_out, 1)
                if c.live:
                    dve.wait_ge(x2T_hi_done, count(c, 1, 1))
                    low(x2T_lo[:, :, :], turn0, x2T_hi[:, :, :], x2T_lo_done)
                    gated_linear(c, 0, score_ps[:, 0, :], score_ps[:, 1, :])
                    gated_linear(c, 1, score_ps[:, 2, :], score_ps[:, 3, :])
                if b.live:
                    attention_out(b, 1)
                if c.live:
                    gated_linear(c, 2, turn0[:, :], turn1[:, :])

            steps(dve, step)


_INS = ["L0_attn_x", "L0_attn_w_attn", "L0_attn_w_proj", "L0_ffn_w_gate", "L0_ffn_w_up", "L0_ffn_w_down"]


def kernel(**inputs):
    import numpy as _np
    import concourse.bacc as _bacc
    from concourse import mybir as _mybir
    from concourse.bass_utils import run_bass_kernel_spmd as _run

    nc = _bacc.Bacc("TRN2", target_bir_lowering=False, num_devices=1)
    arrays, args = {}, []
    for name in _INS:
        a = _np.ascontiguousarray(inputs[name])
        arrays[f"in_{name}_dram"] = a
        args.append(nc.dram_tensor(f"in_{name}_dram", a.shape, _mybir.dt.from_np(a.dtype), kind="ExternalInput").ap())
    out = nc.dram_tensor("out_dram", inputs["L0_attn_x"].shape, _mybir.dt.float32, kind="ExternalOutput").ap()
    sandwich_block(nc, *args, out)
    return _run(nc, [arrays], core_ids=[0]).results[0]["out_dram"]
```

```python
import concourse.bass as bass
from concourse import mybir
from contextlib import ExitStack


def sandwich_block(nc, x_in, w_attn, w_proj, w_gate, w_up, w_down, out):
    f32, f32r, i32 = mybir.dt.float32, mybir.dt.float32r, mybir.dt.int32
    ALU = mybir.AluOpType
    ACT = mybir.ActivationFunctionType
    AX = mybir.AxisListType

    B, T, C = x_in.shape
    P = 128
    HEADS, WIN = 16, 64
    D = C // HEADS
    CB = C // P
    TT = 2
    GT = TT * P
    NG = B * T // GT
    HID = w_gate.shape[0]
    HB = HID // P
    HP = HB // 2
    PAIRS = HEADS // 2
    VW = 2 * (D + 1)
    LN_EPS = 1e-5
    Q_SCALE = D ** -0.5
    INT_SCALE = 1.0 / 127.0
    H_SCALE = 0.5 * INT_SCALE ** 3

    x_v = x_in.rearrange("b t c -> (b t) c").rearrange("(g t p) c -> g p t c", t=TT, p=P)
    out_v = out.rearrange("b t c -> (b t) c").rearrange("(g t p) c -> g p t c", t=TT, p=P)

    ctx = ExitStack()
    with ctx:
        def sb(name, shape, dt=f32):
            return ctx.enter_context(nc.sbuf_tensor(name, shape, dt))

        def pb(name, shape):
            return ctx.enter_context(nc.psum_tensor(name, shape, f32))

        def sem(name):
            return ctx.enter_context(nc.semaphore(name))

        wa_hi, wa_lo = sb("wa_hi", [P, CB, 3 * C], f32r), sb("wa_lo", [P, CB, 3 * C], f32r)
        wp_hi, wp_lo = sb("wp_hi", [P, CB, C], f32r), sb("wp_lo", [P, CB, C], f32r)
        wg_hi, wg_lo = sb("wg_hi", [P, CB, HID], f32r), sb("wg_lo", [P, CB, HID], f32r)
        wu_hi, wu_lo = sb("wu_hi", [P, CB, HID], f32r), sb("wu_lo", [P, CB, HID], f32r)
        wd_hi, wd_lo = sb("wd_hi", [P, HB, C], f32r), sb("wd_lo", [P, HB, C], f32r)
        wa_raw, wp_raw = sb("wa_raw", [P, 3 * CB, C]), sb("wp_raw", [P, CB, C])
        wg_int, wu_int = sb("wg_int", [P, HB, C], i32), sb("wu_int", [P, HB, C], i32)
        wd_int = sb("wd_int", [P, CB, HID], i32)
        wg_raw, wu_raw, wd_raw = sb("wg_raw", [P, HB, C]), sb("wu_raw", [P, HB, C]), sb("wd_raw", [P, CB, HID])
        ident = sb("ident", [P, P])
        even_head, odd_head = sb("even_head", [P, 1]), sb("odd_head", [P, 1])
        minus_half = sb("minus_half", [P, TT])
        low_sizes, low_scratch = sb("low_sizes", [P, 3]), sb("low_scratch", [P, CB, HID])
        ones_col = sb("ones_col", [P, 1])
        any_low = sb("any_low", [1, 1], i32)

        x_sb = [sb(f"x_sb{i}", [P, TT, C]) for i in range(2)]
        x_res = [sb(f"x_res{i}", [P, TT, C]) for i in range(2)]
        x2 = [sb(f"x2_{i}", [P, TT, C]) for i in range(2)]
        out_sb = [sb(f"out_sb{i}", [P, TT, C]) for i in range(2)]
        xn, x2n = sb("xn", [P, TT, C]), sb("x2n", [P, TT, C])
        xT_hi, xT_lo = sb("xT_hi", [P, CB, GT], f32r), sb("xT_lo", [P, CB, GT], f32r)
        x2T_hi, x2T_lo = sb("x2T_hi", [P, CB, GT], f32r), sb("x2T_lo", [P, CB, GT], f32r)
        yT_hi, yT_lo = sb("yT_hi", [P, CB, GT], f32r), sb("yT_lo", [P, CB, GT], f32r)
        qT = sb("qT", [P, CB, GT])
        kT = sb("kT", [P, CB, 2, GT])
        v_sb = sb("v_sb", [P, 2, 2, D + 1, TT, PAIRS])
        v_stage = sb("v_stage", [P, 2, D, TT, PAIRS])
        probs = [sb(f"probs{t}", [P, HEADS * WIN]) for t in range(TT)]
        score_max = [sb(f"score_max{t}", [P, HEADS]) for t in range(TT)]
        pT = sb("pT", [P, 2 * TT, 4, P])
        inv_sum = sb("inv_sum", [P, HEADS])
        y_sb = sb("y_sb", [P, TT, C])
        attn_sb, ffn_sb = sb("attn_sb", [P, TT, C]), sb("ffn_sb", [P, TT, C])
        tanh_sb, gated, h_sb = (sb(n, [P, HP, 2 * GT]) for n in ("tanh_sb", "gated", "h_sb"))
        hT_hi, hT_lo = sb("hT_hi", [P, HP, 2, GT], f32r), sb("hT_lo", [P, HP, 2, GT], f32r)
        NORMS = ("in", "attn", "mid", "ffn")
        ACT_NORMS = ("in", "ffn")
        SCALE_STEPS = {n: 2 if n in ACT_NORMS else 1 for n in NORMS}
        stats = {n: sb(f"stats_{n}", [P, TT, 6]) for n in NORMS}
        mean_var = {n: sb(f"mean_var_{n}", [P, TT, 2]) for n in NORMS}
        neg_mean = {n: sb(f"neg_mean_{n}", [P, TT]) for n in ACT_NORMS}
        var_eps = {n: sb(f"var_eps_{n}", [P, TT]) for n in NORMS}
        rstd = {n: sb(f"rstd_{n}", [P, TT]) for n in NORMS}
        neg_mr = {n: sb(f"neg_mr_{n}", [P, TT]) for n in ACT_NORMS}

        score_ps = pb("score_ps", [P, 4, 512])
        turn0, turn1 = pb("turn0", [P, 512]), pb("turn1", [P, 512])
        pT_ps, y_ps = pb("pT_ps", [P, 512]), pb("y_ps", [P, 512])

        w_loaded = [sem(f"w_loaded{i}") for i in range(5)]
        ident_set, masks_set, ones_set = sem("ident_set"), sem("masks_set"), sem("ones_set")
        gate_cast, up_down_cast = sem("gate_cast"), sem("up_down_cast")
        low_sized, low_summed, any_low_set = sem("low_sized"), sem("low_summed"), sem("any_low_set")
        wT_done, wT_hi_done, wT_lo_done = sem("wT_done"), sem("wT_hi_done"), sem("wT_lo_done")
        x_loaded = [sem(f"x_loaded{i}") for i in range(2)]
        x_kept = [sem(f"x_kept{i}") for i in range(2)]
        stored = [sem(f"stored{i}") for i in range(2)]
        norm_steps = {n: sem(f"norm_steps_{n}") for n in NORMS}
        norm_scales = {n: sem(f"norm_scales_{n}") for n in NORMS}
        normed = {n: sem(f"normed_{n}") for n in NORMS}
        xT_done, xT_hi_done, xT_lo_done = sem("xT_done"), sem("xT_hi_done"), sem("xT_lo_done")
        yT_done, yT_hi_done, yT_lo_done = sem("yT_done"), sem("yT_hi_done"), sem("yT_lo_done")
        x2T_done, x2T_hi_done, x2T_lo_done = sem("x2T_done"), sem("x2T_hi_done"), sem("x2T_lo_done")
        q_done, k_done, v_done = sem("q_done"), sem("k_done"), sem("v_done")
        q_out, k_even_out, k_odd_out = sem("q_out"), sem("k_even_out"), sem("k_odd_out")
        v_out, v_placed = sem("v_out"), sem("v_placed")
        scores_done = sem("scores_done")
        softmax_steps = sem("softmax_steps")
        exp_done = sem("exp_done")
        pT_done, pT_out, pv_done = sem("pT_done"), sem("pT_out"), sem("pv_done")
        y_steps = sem("y_steps")
        proj_done, attn_out, x2_done = sem("proj_done"), sem("attn_out"), sem("x2_done")
        gate_done, up_done = sem("gate_done"), sem("up_done")
        tanh_done, glu_steps = sem("tanh_done"), sem("glu_steps")
        h_hi_done, h_lo_done = sem("h_hi_done"), sem("h_lo_done")
        down_done, ffn_out, out_done = sem("down_done"), sem("ffn_out"), sem("out_done")

        class Group:

            def __init__(self, k, c):
                self.k, self.c = k, c
                self.number, self.parity, self.half = 2 * k + c, c % 2, k + c // 2
                self.live = not isinstance(k, int) or 0 <= 2 * k + c < NG

            def shift(self, by):
                return Group(self.k, self.c + by)

        def count(g, each, k):
            return g.number * each + k

        def nth(g, k=1):
            return (g.half + k) * 16

        def ahead(eng, *values):
            for v in values:
                if not isinstance(v, int):
                    eng.compute_val(v)

        LOOP_FROM, LOOP_TO = 4, NG - 4
        assert NG % 2 == 0

        FLAG_STEP = 2

        def first_steps(step):
            for s in range(-1, LOOP_FROM):
                step(Group(0, s))

        def other_steps(eng, step):
            with eng.Fori(LOOP_FROM // 2, LOOP_TO // 2) as k:
                step(Group(k, 0))
                step(Group(k, 1))
            for s in range(LOOP_TO, NG + 2):
                step(Group(0, s))

        def steps(eng, step):
            first_steps(step)
            other_steps(eng, step)

        def at_flag(s):
            return isinstance(s.k, int) and s.number == FLAG_STEP

        HALVES = (slice(0, WIN), slice(WIN, P))

        block = ctx.enter_context(nc.Block())

        def weight_turns():
            turns = []
            for raw, hi, lo, n in ((wa_raw, wa_hi, wa_lo, 3 * CB), (wp_raw, wp_hi, wp_lo, CB),
                                   (wg_raw, wg_hi, wg_lo, HB), (wu_raw, wu_hi, wu_lo, HB)):
                for r in range(0, n, 2):
                    blocks = [raw[:, r + i, c * P:(c + 1) * P] for c in range(CB) for i in range(2)]
                    turns.append((raw, blocks, hi[:, :, r * P:(r + 2) * P], lo[:, :, r * P:(r + 2) * P]))
            for b in range(0, HB, 2):
                blocks = [wd_raw[:, r, (b + i) * P:(b + i + 1) * P] for i in range(2) for r in range(CB)]
                turns.append((wd_raw, blocks, wd_hi[:, b:b + 2, :], wd_lo[:, b:b + 2, :]))
            return turns

        TURNS = weight_turns()
        W_BANKS = [turn0, turn1, pT_ps, y_ps]

        @block.sync
        def _(sp):
            def load(g):
                ahead(sp, g.number, nth(g, 0), count(g.shift(-2), 1, 1))
                if g.shift(-2).live:
                    sp.wait_ge(x_kept[g.parity], nth(g, 0))
                    sp.wait_ge(normed["in"], count(g.shift(-2), 1, 1))
                sp.dma_start(x_sb[g.parity][:, :, :], x_v[g.number, :, :, :]).then_inc(x_loaded[g.parity], 16)

            load(Group(0, 0))
            sp.dma_start(wa_raw[:, :, :], w_attn.rearrange("(r p) c -> p r c", p=P)).then_inc(w_loaded[0], 16)
            sp.dma_start(wp_raw[:, :, :], w_proj.rearrange("(r p) c -> p r c", p=P)).then_inc(w_loaded[1], 16)
            sp.dma_start(wg_int[:, :, :], w_gate.rearrange("(r p) c -> p r c", p=P)).then_inc(w_loaded[2], 16)
            sp.dma_start(wu_int[:, :, :], w_up.rearrange("(r p) c -> p r c", p=P)).then_inc(w_loaded[3], 16)
            sp.dma_start(wd_int[:, :, :], w_down.rearrange("(r p) c -> p r c", p=P)).then_inc(w_loaded[4], 16)

            load(Group(0, 1))

            def step(s):
                a, b, e = s.shift(1), s, s.shift(-2)
                if b.live:
                    ahead(sp, count(b, 1, 1))
                    sp.wait_ge(v_out, count(b, 1, 1))
                    for w, tokens in enumerate(HALVES):
                        for side, place in enumerate(HALVES):
                            sp.dma_start(v_sb[place, w, side, 0:D, :, :], v_stage[tokens, side, :, :, :])\
                              .then_inc(v_placed, 16)
                if a.live:
                    ahead(sp, nth(a), count(a.shift(-2), 1, 1))
                    sp.wait_ge(x_loaded[a.parity], nth(a))
                    if a.shift(-2).live:
                        sp.wait_ge(x2_done, count(a.shift(-2), 1, 1))
                    sp.dma_start(x_res[a.parity][:, :, :], x_sb[a.parity][:, :, :])\
                      .then_inc(x_kept[a.parity], 16)
                if e.live:
                    ahead(sp, e.number, count(e, 1, 1))
                    sp.wait_ge(out_done, count(e, 1, 1))
                    sp.dma_start(out_v[e.number, :, :, :], out_sb[e.parity][:, :, :])\
                      .then_inc(stored[e.parity], 16)
                if a.shift(2).live and a.live:
                    load(a.shift(2))

            steps(sp, step)
            for i in range(2):
                sp.wait_ge(stored[i], NG // 2 * 16)

        @block.gpsimd
        def _(pool):
            pool.memset(ident[:, :], 0.0).then_inc(ident_set, 1)
            pool.memset(minus_half[:, :], -0.5).then_inc(ones_set, 1)
            pool.wait_ge(ident_set, 1)
            pool.affine_select(out=ident[:, :], in_=ident[:, :], compare_op=ALU.not_equal, fill=1.0,
                               base=0, pattern=[[-1, P]], channel_multiplier=1).then_inc(ident_set, 1)
            pool.memset(v_sb[:, :, :, :, :, :], 0.0).then_inc(ones_set, 1)
            pool.memset(ones_col[:, :], 1.0).then_inc(ones_set, 1)
            pool.wait_ge(ones_set, 3)
            pool.memset(v_sb[0:WIN, :, 0, D:D + 1, :, :], 1.0).then_inc(ones_set, 1)
            pool.memset(v_sb[WIN:P, :, 1, D:D + 1, :, :], 1.0).then_inc(ones_set, 1)
            pool.wait_ge(ones_set, 5)

            def scales(norm, g):
                pool.wait_ge(norm_steps[norm], count(g, 3, 3))
                if g.shift(-1).live:
                    pool.wait_ge(normed[norm], count(g.shift(-1), 1, 1))
                pool.tensor_tensor(rstd[norm][:, :], var_eps[norm][:, :], minus_half[:, :], ALU.pow)\
                    .then_inc(norm_scales[norm], 1)
                if norm not in ACT_NORMS:
                    return
                pool.wait_ge(norm_scales[norm], count(g, 2, 1))
                pool.tensor_tensor(neg_mr[norm][:, :], neg_mean[norm][:, :], rstd[norm][:, :], ALU.mult)\
                    .then_inc(norm_scales[norm], 1)

            def h_low(g, j):
                pool.wait_ge(h_hi_done, count(g, HP, j + 1))
                pool.tensor_tensor(hT_lo[:, j, :, :], h_sb[:, j, :].rearrange("p (b t) -> p b t", b=2),
                                   hT_hi[:, j, :, :].bitcast(f32), ALU.subtract).then_inc(h_lo_done, 1)

            def step(s):
                f, c, e = s.shift(2), s.shift(-1), s.shift(-2)
                if c.live:
                    scales("attn", c)
                if c.live:
                    scales("mid", c)
                if f.live:
                    scales("in", f)
                if e.live:
                    scales("ffn", e)
                if c.live:
                    for j in range(HP):
                        h_low(c, j)

            step(Group(0, -2))
            steps(pool, step)

        @block.tensor
        def _(pe):
            pe.wait_ge(ident_set, 2)
            for n, (raw, blocks, _, _) in enumerate(TURNS):
                if raw is wa_raw or raw is wp_raw:
                    pe.wait_ge(w_loaded[0 if raw is wa_raw else 1], 16)
                elif raw is wg_raw:
                    pe.wait_ge(gate_cast, 1)
                else:
                    pe.wait_ge(up_down_cast, 1 if raw is wu_raw else 2)
                if n >= len(W_BANKS):
                    pe.wait_ge(wT_lo_done, n + 1 - len(W_BANKS))
                bank = W_BANKS[n % len(W_BANKS)]
                for i, b in enumerate(blocks):
                    mm = pe.transpose(bank[:, i * P:(i + 1) * P], b, ident[:, :])
                mm.then_inc(wT_done, 1)
            pe.wait_ge(wT_lo_done, len(TURNS))
            pe.wait_ge(ones_set, 5)

            def turn_tokens(bank, src, done):
                for c in range(CB):
                    for t in range(TT):
                        mm = pe.transpose(bank[:, c * GT + t * P:c * GT + (t + 1) * P],
                                          src[:, t, c * P:(c + 1) * P], ident[:, :])
                mm.then_inc(done, 1)

            def split_product(out_ap, stationary, moving, blocks, skip=None):
                n = len(blocks)
                for i, blk in enumerate(blocks):
                    (s_hi, s_lo), (m_hi, m_lo) = stationary(blk), moving(blk)
                    products = [(s_hi, m_hi)]
                    if skip != "moving":
                        products.append((s_hi, m_lo))
                    if skip != "stationary":
                        products.append((s_lo, m_hi))
                    for k, (x, y) in enumerate(products):
                        mm = pe.matmul(out_ap, x, y, start=(i == 0 and k == 0),
                                       stop=(i == n - 1 and k == len(products) - 1))
                return mm

            def q_or_k(bank, first_block, done):
                for m in range(CB):
                    col = (first_block + m) * P
                    mm = split_product(bank[:, m * GT:(m + 1) * GT],
                                       lambda c: (wa_hi[:, c, col:col + P], wa_lo[:, c, col:col + P]),
                                       lambda c: (xT_hi[:, c, :], xT_lo[:, c, :]), range(CB))
                mm.then_inc(done, 1)

            def values():
                for t in range(TT):
                    mm = split_product(turn1[:, t * C:(t + 1) * C],
                                       lambda c: (xT_hi[:, c, t * P:(t + 1) * P], xT_lo[:, c, t * P:(t + 1) * P]),
                                       lambda c: (wa_hi[:, c, 2 * C:3 * C], wa_lo[:, c, 2 * C:3 * C]),
                                       range(CB))
                mm.then_inc(v_done, 1)

            def scores(t, m):
                for w in range(2):
                    at = t * P + w * WIN
                    for b in range(4):
                        mm = pe.matmul(score_ps[w * WIN:(w + 1) * WIN, b, m * P:(m + 1) * P],
                                       qT[32 * b:32 * b + 32, m, at:at + WIN],
                                       kT[32 * b:32 * b + 32, m, :, at:at + WIN],
                                       start=True, stop=True)
                if m == CB - 1:
                    mm.then_inc(scores_done, 1)

            def turn_probs(g, t, m):
                unit = 2 * t + m
                if m == 0:
                    pe.wait_ge(exp_done, count(g, TT, t + 1))
                if unit or g.shift(-1).live:
                    pe.wait_ge(pT_out, count(g, 4, unit))
                for b in range(4):
                    at = (2 * b + m) * P
                    mm = pe.transpose(pT_ps[:, b * P:(b + 1) * P], probs[t][:, at:at + P], ident[:, :])
                mm.then_inc(pT_done, 1)

            def weigh_values(g, t, m):
                unit = 2 * t + m
                pe.wait_ge(pT_out, count(g, 4, unit + 1))
                if unit == 0:
                    pe.wait_ge(v_placed, count(g, 64, 64))
                if m == 0 and (t or g.shift(-1).live):
                    pe.wait_ge(y_steps, count(g, 4, 2 * t))
                for b in range(4):
                    pair = 4 * m + b
                    for w in range(2):
                        mm = pe.matmul(y_ps[w * WIN:(w + 1) * WIN, pair * VW:(pair + 1) * VW],
                                       pT[:, unit, b, w * WIN:(w + 1) * WIN],
                                       v_sb[:, w, :, :, t, pair], start=True, stop=True)
                mm.then_inc(pv_done, 1)

            def project():
                for t in range(TT):
                    mm = split_product(turn0[:, t * C:(t + 1) * C],
                                       lambda c: (yT_hi[:, c, t * P:(t + 1) * P], yT_lo[:, c, t * P:(t + 1) * P]),
                                       lambda c: (wp_hi[:, c, :], wp_lo[:, c, :]), range(CB))
                mm.then_inc(proj_done, 1)

            def hidden(bank, hi, lo, j, done, low):
                for i in range(2):
                    col = (2 * j + i) * P
                    mm = split_product(bank[:, i * GT:(i + 1) * GT],
                                       lambda c: (hi[:, c, col:col + P], lo[:, c, col:col + P]),
                                       lambda c: (x2T_hi[:, c, :], x2T_lo[:, c, :]), range(CB),
                                       skip=None if low else "stationary")
                mm.then_inc(done, 1)

            def down(low):
                for t in range(TT):
                    def h_of(x, k):
                        return x[:, k // 2, k % 2, t * P:(t + 1) * P]
                    mm = split_product(turn0[:, t * C:(t + 1) * C],
                                       lambda k: (h_of(hT_hi, k), h_of(hT_lo, k)),
                                       lambda k: (wd_hi[:, k, :], wd_lo[:, k, :]), range(HB),
                                       skip=None if low else "moving")
                mm.then_inc(down_done, 1)

            def sum_low_sizes():
                pe.wait_ge(low_sized, 3)
                pe.matmul(y_ps[0:1, 0:3], ones_col[:, :], low_sizes[:, :], start=True, stop=True)\
                  .then_inc(low_summed, 1)

            def step(s, low=True):
                a, b, c, e = s.shift(1), s, s.shift(-1), s.shift(-2)
                if b.live:
                    pe.wait_ge(q_out, count(b, 1, 1))
                    pe.wait_ge(k_even_out, count(b, 1, 1))
                    pe.wait_ge(k_odd_out, count(b, 1, 1))
                    if e.live:
                        pe.wait_ge(glu_steps, count(e, 2 * HP, 4))
                    elif c.live:
                        pe.wait_ge(softmax_steps, count(c, 4, 4))
                    scores(0, 0)
                if c.live:
                    pe.wait_ge(y_steps, count(c, 4, 4))
                    if e.live:
                        pe.wait_ge(glu_steps, count(e, 2 * HP, 5))
                    turn_tokens(turn0, y_sb, yT_done)
                if b.live:
                    scores(0, 1)
                if at_flag(s):
                    sum_low_sizes()
                if b.live:
                    if e.live:
                        pe.wait_ge(glu_steps, count(e, 2 * HP, 6))
                    elif c.live:
                        pe.wait_ge(k_even_out, count(b, 1, 1))
                        pe.wait_ge(k_odd_out, count(b, 1, 1))
                    values()
                if c.live:
                    pe.wait_ge(yT_lo_done, count(c, 1, 1))
                    project()
                if a.live:
                    pe.wait_ge(normed["in"], count(a, 1, 1))
                    if b.live:
                        pe.wait_ge(v_out, count(b, 1, 1))
                    turn_tokens(turn1, xn, xT_done)
                if b.live:
                    pe.wait_ge(softmax_steps, count(b, 4, 2))
                    scores(1, 0)
                    scores(1, 1)
                if e.live:
                    pe.wait_ge(h_lo_done, count(e, HP, HP))
                    if c.live:
                        pe.wait_ge(attn_out, count(c, 1, 1))
                    else:
                        pe.wait_ge(glu_steps, count(e, 2 * HP, 5))
                    down(low)
                if b.live:
                    turn_probs(b, 0, 0)
                if a.live:
                    pe.wait_ge(xT_lo_done, count(a, 1, 1))
                    q_or_k(turn1, 0, q_done)
                if b.live:
                    turn_probs(b, 0, 1)
                    if at_flag(s):
                        pe.wait_ge(any_low_set, 2)
                    weigh_values(b, 0, 0)
                if c.live:
                    pe.wait_ge(normed["mid"], count(c, 1, 1))
                    if e.live:
                        pe.wait_ge(ffn_out, count(e, 1, 1))
                    else:
                        pe.wait_ge(attn_out, count(c, 1, 1))
                    turn_tokens(turn0, x2n, x2T_done)
                if b.live:
                    weigh_values(b, 0, 1)
                if a.live:
                    pe.wait_ge(q_out, count(a, 1, 1))
                    q_or_k(turn1, CB, k_done)
                if b.live:
                    turn_probs(b, 1, 0)
                if c.live:
                    pe.wait_ge(x2T_lo_done, count(c, 1, 1))
                if c.live:
                    if b.live:
                        pe.wait_ge(softmax_steps, count(b, 4, 4))
                    else:
                        pe.wait_ge(glu_steps, count(e, 2 * HP, 4))
                    hidden(score_ps[:, 0, :], wg_hi, wg_lo, 0, gate_done, low)
                    hidden(score_ps[:, 1, :], wu_hi, wu_lo, 0, up_done, low)
                if b.live:
                    turn_probs(b, 1, 1)
                    weigh_values(b, 1, 0)
                if c.live:
                    hidden(score_ps[:, 2, :], wg_hi, wg_lo, 1, gate_done, low)
                    hidden(score_ps[:, 3, :], wu_hi, wu_lo, 1, up_done, low)
                if b.live:
                    weigh_values(b, 1, 1)
                if c.live:
                    hidden(turn0, wg_hi, wg_lo, 2, gate_done, low)
                    if a.live:
                        pe.wait_ge(k_even_out, count(a, 1, 1))
                        pe.wait_ge(k_odd_out, count(a, 1, 1))
                    elif b.live:
                        pe.wait_ge(v_out, count(b, 1, 1))
                    else:
                        pe.wait_ge(glu_steps, count(e, 2 * HP, 6))
                    hidden(turn1, wu_hi, wu_lo, 2, up_done, low)

            first_steps(step)
            pe.wait_ge(any_low_set, 2)
            flag = pe.value_load(any_low[0:1, 0:1], min_val=0, max_val=1)
            with pe.If(flag > 0):
                other_steps(pe, lambda s: step(s, low=True))
            with pe.Else():
                other_steps(pe, lambda s: step(s, low=False))

        @block.scalar
        def _(act):
            def split(x):
                return x.rearrange("p (a b) -> p a b", a=2)

            def copy(to, of, done, scale=1.0):
                act.activation(to, of, ACT.Copy, scale=scale).then_inc(done, 1)

            def normalise(norm, g, to, of):
                act.wait_ge(norm_scales[norm], count(g, 2, 2))
                for t in range(TT):
                    last = act.activation(to[:, t, :], of[:, t, :], ACT.Identity,
                                          scale=rstd[norm][:, t:t + 1], bias=neg_mr[norm][:, t:t + 1])
                last.then_inc(normed[norm], 1)

            def values_out(g):
                act.wait_ge(v_done, count(g, 1, 1))
                copy(v_stage[:, :, :, :, :].rearrange("p e d t h -> p e d (t h)"),
                     turn1[:, :].rearrange("p (n e d) -> p e d n", e=2, d=D), v_out)

            def exponentials(g, t):
                act.wait_ge(softmax_steps, count(g, 4, 2 * t + 2))
                act.activation(probs[t][:, :], probs[t][:, :], ACT.Exp).then_inc(exp_done, 1)

            def probs_out(g, unit):
                act.wait_ge(pT_done, count(g, 4, unit + 1))
                copy(pT[:, unit, :, :], pT_ps[:, :].rearrange("p (b i) -> p b i", b=4), pT_out)

            def tanh(g, j, bank):
                act.wait_ge(gate_done, count(g, HP, j + 1))
                act.activation(tanh_sb[:, j, :], bank, ACT.Tanh, scale=0.5 * INT_SCALE).then_inc(tanh_done, 1)

            def h_high(g, j):
                act.wait_ge(glu_steps, count(g, 2 * HP, 2 * j + 2))
                if j == 0 and g.shift(-1).live:
                    act.wait_ge(down_done, count(g.shift(-1), 1, 1))
                copy(hT_hi[:, j, :, :], split(h_sb[:, j, :]), h_hi_done)

            def size_low_part(i):
                lo = (wg_lo, wu_lo, wd_lo)[i]
                act.wait_ge(wT_lo_done, len(TURNS))
                if i:
                    act.wait_ge(low_sized, i)
                scratch = low_scratch[:, :, :].rearrange("p a b -> p (a b)")\
                                               .rearrange("p (a b) -> p a b", a=lo.shape[1])
                act.activation(scratch, lo[:, :, :].bitcast(f32), ACT.Abs,
                               accum_out=low_sizes[:, i:i + 1]).then_inc(low_sized, 1)

            def step(s):
                f, a, b, c, e = s.shift(2), s.shift(1), s, s.shift(-1), s.shift(-2)
                first = isinstance(s.k, int) and s.number == -1
                if c.live:
                    act.wait_ge(yT_done, count(c, 1, 1))
                    copy(yT_hi[:, :, :], split(turn0[:, :]), yT_hi_done)
                if e.live:
                    h_high(e, 2)
                if b.live:
                    values_out(b)
                if c.live:
                    act.wait_ge(proj_done, count(c, 1, 1))
                    if c.shift(-1).live:
                        act.wait_ge(x2_done, count(c.shift(-1), 1, 1))
                    copy(attn_sb[:, :, :], split(turn0[:, :]), attn_out)
                if a.live:
                    act.wait_ge(xT_done, count(a, 1, 1))
                    copy(xT_hi[:, :, :], split(turn1[:, :]), xT_hi_done)
                if b.live:
                    exponentials(b, 0)
                if e.live:
                    act.wait_ge(down_done, count(e, 1, 1))
                    if e.shift(-1).live:
                        act.wait_ge(out_done, count(e.shift(-1), 1, 1))
                    copy(ffn_sb[:, :, :], split(turn0[:, :]), ffn_out)
                if b.live:
                    probs_out(b, 0)
                if first:
                    size_low_part(0)
                if a.live:
                    act.wait_ge(q_done, count(a, 1, 1))
                    copy(qT[:, :, :], split(turn1[:, :]), q_out, scale=Q_SCALE)
                if b.live:
                    probs_out(b, 1)
                if c.live:
                    act.wait_ge(x2T_done, count(c, 1, 1))
                    copy(x2T_hi[:, :, :], split(turn0[:, :]), x2T_hi_done)
                if b.live:
                    exponentials(b, 1)
                if first:
                    size_low_part(1)
                if a.live:
                    act.wait_ge(k_done, count(a, 1, 1))
                    copy(kT[:, :, 0, :], split(turn1[:, :]), k_even_out, scale=even_head[:, :])
                if b.live:
                    probs_out(b, 2)
                if c.live:
                    tanh(c, 0, score_ps[:, 0, :])
                if f.live:
                    normalise("in", f, xn, x_sb[f.parity])
                if first:
                    size_low_part(2)
                if b.live:
                    probs_out(b, 3)
                if c.live:
                    h_high(c, 0)
                    tanh(c, 1, score_ps[:, 2, :])
                if e.live:
                    normalise("ffn", e, ffn_sb, ffn_sb)
                if c.live:
                    tanh(c, 2, turn0[:, :])
                    h_high(c, 1)

            step(Group(0, -2))
            for n, (raw, _, hi, _) in enumerate(TURNS):
                if raw is wg_raw and TURNS[n - 1][0] is not wg_raw:
                    act.wait_ge(w_loaded[2], 16)
                    copy(wg_raw[:, :, :], wg_int[:, :, :], gate_cast)
                act.wait_ge(wT_done, n + 1)
                copy(hi, split(W_BANKS[n % len(W_BANKS)][:, :]), wT_hi_done)
            act.wait_ge(masks_set, 2)
            steps(act, step)

        @block.vector
        def _(dve):
            def split(x):
                return x.rearrange("p (a b) -> p a b", a=2)

            dve.wait_ge(ident_set, 2)
            head_rows = ident[:, :].rearrange("p (a e d) -> p a e d", e=2, d=D)
            dve.tensor_reduce(even_head[:, :], head_rows[:, :, 0, :], AX.XY, ALU.add).then_inc(masks_set, 1)
            dve.tensor_reduce(odd_head[:, :], head_rows[:, :, 1, :], AX.XY, ALU.add).then_inc(masks_set, 1)
            def low(to, bank, hi, done):
                dve.tensor_tensor(to, split(bank[:, :]), hi.bitcast(f32),
                                  ALU.subtract).then_inc(done, 1)

            def statistics(norm, g, x):
                for t in range(TT):
                    last = dve.bn_stats(stats[norm][:, t, :], x[:, t, :])
                last.then_inc(norm_steps[norm], 1)
                ahead(dve, count(g, 3, 1))
                dve.wait_ge(masks_set, 2)
                dve.wait_ge(norm_steps[norm], count(g, 3, 1))
                for t in range(TT):
                    last = dve.bn_aggr(mean_var[norm][:, t, :], stats[norm][:, t, :])
                last.then_inc(norm_steps[norm], 1)
                dve.wait_ge(norm_steps[norm], count(g, 3, 2))
                if g.shift(-1).live:
                    n = SCALE_STEPS[norm]
                    dve.wait_ge(norm_scales[norm], count(g.shift(-1), n, n))
                if norm in ACT_NORMS:
                    dve.tensor_scalar(neg_mean[norm][:, :], mean_var[norm][:, :, 0], -1.0, None, ALU.mult)
                dve.tensor_scalar(var_eps[norm][:, :], mean_var[norm][:, :, 1], LN_EPS, None,
                                  ALU.add).then_inc(norm_steps[norm], 1)

            def normalise(norm, g, to, of):
                dve.wait_ge(norm_scales[norm], count(g, 1, 1))
                for t in range(TT):
                    last = dve.tensor_scalar(to[:, t, :], of[:, t, :], mean_var[norm][:, t, 0:1],
                                             rstd[norm][:, t:t + 1], ALU.subtract, ALU.mult)
                last.then_inc(normed[norm], 1)

            def maximum(g, t):
                dve.wait_ge(scores_done, count(g, TT, t + 1))
                dve.tensor_reduce(score_max[t][:, :].rearrange("p (b h) -> p b h", b=4),
                                  score_ps[:, :, 0:4 * WIN].rearrange("p b (h j) -> p b h j", j=WIN),
                                  AX.X, ALU.max).then_inc(softmax_steps, 1)

            def less_maximum(g, t):
                dve.wait_ge(softmax_steps, count(g, 4, 2 * t + 1))
                dve.tensor_tensor(probs[t][:, :].rearrange("p (b h j) -> p b h j", b=4, j=WIN),
                                  score_ps[:, :, 0:4 * WIN].rearrange("p b (h j) -> p b h j", j=WIN),
                                  score_max[t][:, :].rearrange("p (b h) -> p b h", b=4).unsqueeze(3)
                                  .broadcast_to([P, 4, 4, WIN]), ALU.subtract).then_inc(softmax_steps, 1)

            def attention_out(g, t):
                y = y_ps[:, 0:HEADS * (D + 1)].rearrange("p (h d) -> p h d", d=D + 1)
                dve.wait_ge(pv_done, count(g, 4, 2 * t + 2))
                dve.reciprocal(inv_sum[:, :], y[:, :, D]).then_inc(y_steps, 1)
                dve.wait_ge(y_steps, count(g, 4, 2 * t + 1))
                dve.tensor_tensor(y_sb[:, t, :].rearrange("p (h d) -> p h d", d=D), y[:, :, 0:D],
                                  inv_sum[:, :].unsqueeze(2).broadcast_to([P, HEADS, D]),
                                  ALU.mult).then_inc(y_steps, 1)

            def gated_linear(g, j, g_bank, u_bank):
                dve.wait_ge(tanh_done, count(g, HP, j + 1))
                dve.scalar_tensor_tensor(out=gated[:, j, :], in0=tanh_sb[:, j, :], scalar=1.0, in1=g_bank,
                                         op0=ALU.add, op1=ALU.mult).then_inc(glu_steps, 1)
                dve.wait_ge(glu_steps, count(g, 2 * HP, 2 * j + 1))
                dve.wait_ge(up_done, count(g, HP, j + 1))
                if g.shift(-1).live:
                    dve.wait_ge(h_lo_done, count(g.shift(-1), HP, j + 1))
                dve.scalar_tensor_tensor(out=h_sb[:, j, :], in0=u_bank, scalar=H_SCALE, in1=gated[:, j, :],
                                         op0=ALU.mult, op1=ALU.mult).then_inc(glu_steps, 1)

            def set_flag():
                dve.wait_ge(low_summed, 1)
                dve.tensor_scalar(low_sizes[0:1, :], y_ps[0:1, 0:3], 0.0, None, ALU.is_gt).then_inc(any_low_set, 1)
                dve.wait_ge(any_low_set, 1)
                dve.tensor_reduce(any_low[:, :], low_sizes[0:1, :], AX.X, ALU.max).then_inc(any_low_set, 1)

            def step(s):
                f, a, b, c, e = s.shift(2), s.shift(1), s, s.shift(-1), s.shift(-2)
                if at_flag(s):
                    set_flag()
                if c.live:
                    dve.wait_ge(yT_hi_done, count(c, 1, 1))
                    low(yT_lo[:, :, :], turn0, yT_hi[:, :, :], yT_lo_done)
                if b.live:
                    maximum(b, 0)
                    less_maximum(b, 0)
                if c.live:
                    dve.wait_ge(attn_out, count(c, 1, 1))
                    statistics("attn", c, attn_sb)
                if a.live:
                    dve.wait_ge(xT_hi_done, count(a, 1, 1))
                    low(xT_lo[:, :, :], turn1, xT_hi[:, :, :], xT_lo_done)
                if c.live:
                    normalise("attn", c, attn_sb, attn_sb)
                    dve.wait_ge(normed["attn"], count(c, 1, 1))
                    dve.wait_ge(x_kept[c.parity], nth(c))
                    if c.shift(-2).live:
                        dve.wait_ge(out_done, count(c.shift(-2), 1, 1))
                    dve.tensor_tensor(x2[c.parity][:, :, :], attn_sb[:, :, :], x_res[c.parity][:, :, :],
                                      ALU.add).then_inc(x2_done, 1)
                    dve.wait_ge(x2_done, count(c, 1, 1))
                    statistics("mid", c, x2[c.parity])
                if b.live:
                    maximum(b, 1)
                if c.live:
                    normalise("mid", c, x2n, x2[c.parity])
                if b.live:
                    less_maximum(b, 1)
                if c.live:
                    dve.wait_ge(x2T_hi_done, count(c, 1, 1))
                    low(x2T_lo[:, :, :], turn0, x2T_hi[:, :, :], x2T_lo_done)
                if b.live:
                    attention_out(b, 0)
                if f.live:
                    dve.wait_ge(x_loaded[f.parity], nth(f))
                    statistics("in", f, x_sb[f.parity])
                if a.live:
                    dve.wait_ge(k_even_out, count(a, 1, 1))
                    dve.tensor_scalar(kT[:, :, 1, :], split(turn1[:, :]), odd_head[:, :], None,
                                      ALU.mult).then_inc(k_odd_out, 1)
                if c.live:
                    gated_linear(c, 0, score_ps[:, 0, :], score_ps[:, 1, :])
                if e.live:
                    dve.wait_ge(ffn_out, count(e, 1, 1))
                    statistics("ffn", e, ffn_sb)
                if c.live:
                    gated_linear(c, 1, score_ps[:, 2, :], score_ps[:, 3, :])
                if b.live:
                    attention_out(b, 1)
                if c.live:
                    gated_linear(c, 2, turn0[:, :], turn1[:, :])
                if e.live:
                    dve.wait_ge(normed["ffn"], count(e, 1, 1))
                    if e.shift(-2).live:
                        dve.wait_ge(stored[e.parity], nth(e, 0))
                    dve.tensor_tensor(out_sb[e.parity][:, :, :], ffn_sb[:, :, :], x2[e.parity][:, :, :],
                                      ALU.add).then_inc(out_done, 1)

            step(Group(0, -2))
            for n, (raw, _, hi, lo) in enumerate(TURNS):
                if raw is wg_raw and TURNS[n - 1][0] is not wg_raw:
                    for i, (to, of) in enumerate(((wu_raw, wu_int), (wd_raw, wd_int))):
                        dve.wait_ge(w_loaded[3 + i], 16)
                        dve.tensor_copy(to[:, :, :], of[:, :, :]).then_inc(up_down_cast, 1)
                dve.wait_ge(wT_hi_done, n + 1)
                low(lo, W_BANKS[n % len(W_BANKS)], hi, wT_lo_done)
            dve.wait_ge(ones_set, 5)
            steps(dve, step)


_INS = ["L0_attn_x", "L0_attn_w_attn", "L0_attn_w_proj", "L0_ffn_w_gate", "L0_ffn_w_up", "L0_ffn_w_down"]


def kernel(**inputs):
    import numpy as _np
    import concourse.bacc as _bacc
    from concourse import mybir as _mybir
    from concourse.bass_utils import run_bass_kernel_spmd as _run

    nc = _bacc.Bacc("TRN2", target_bir_lowering=False, num_devices=1)
    arrays, args = {}, []
    for name in _INS:
        a = _np.ascontiguousarray(inputs[name])
        arrays[f"in_{name}_dram"] = a
        args.append(nc.dram_tensor(f"in_{name}_dram", a.shape, _mybir.dt.from_np(a.dtype), kind="ExternalInput").ap())
    out = nc.dram_tensor("out_dram", inputs["L0_attn_x"].shape, _mybir.dt.float32, kind="ExternalOutput").ap()
    sandwich_block(nc, *args, out)
    return _run(nc, [arrays], core_ids=[0]).results[0]["out_dram"]
```

```python
import concourse.bass as bass
from concourse import mybir
from contextlib import ExitStack


def sandwich_block(nc, x_in, w_attn, w_proj, w_gate, w_up, w_down, out):
    f32, f32r, i32 = mybir.dt.float32, mybir.dt.float32r, mybir.dt.int32
    ALU = mybir.AluOpType
    ACT = mybir.ActivationFunctionType
    AX = mybir.AxisListType

    B, T, C = x_in.shape
    P = 128
    HEADS, WIN = 16, 64
    D = C // HEADS
    CB = C // P
    TT = 2
    GT = TT * P
    NG = B * T // GT
    HID = w_gate.shape[0]
    HB = HID // P
    HP = HB // 2
    PAIRS = HEADS // 2
    LN_EPS = 1e-5
    Q_SCALE = D ** -0.5
    INT_SCALE = 1.0 / 127.0
    H_SCALE = 0.5 * INT_SCALE ** 3

    x_v = x_in.rearrange("b t c -> (b t) c").rearrange("(g t p) c -> g p t c", t=TT, p=P)
    out_v = out.rearrange("b t c -> (b t) c").rearrange("(g t p) c -> g p t c", t=TT, p=P)

    ctx = ExitStack()
    with ctx:
        def sb(name, shape, dt=f32):
            return ctx.enter_context(nc.sbuf_tensor(name, shape, dt))

        def pb(name, shape):
            return ctx.enter_context(nc.psum_tensor(name, shape, f32))

        def sem(name):
            return ctx.enter_context(nc.semaphore(name))

        wa_hi, wa_lo = sb("wa_hi", [P, CB, 3 * C], f32r), sb("wa_lo", [P, CB, 3 * C], f32r)
        wp_hi, wp_lo = sb("wp_hi", [P, CB, C], f32r), sb("wp_lo", [P, CB, C], f32r)
        wg_hi, wg_lo = sb("wg_hi", [P, CB, HID], f32r), sb("wg_lo", [P, CB, HID], f32r)
        wu_hi, wu_lo = sb("wu_hi", [P, CB, HID], f32r), sb("wu_lo", [P, CB, HID], f32r)
        wd_hi, wd_lo = sb("wd_hi", [P, HB, C], f32r), sb("wd_lo", [P, HB, C], f32r)
        wa_raw, wp_raw = sb("wa_raw", [P, 3 * CB, C]), sb("wp_raw", [P, CB, C])
        wg_int, wu_int = sb("wg_int", [P, HB, C], i32), sb("wu_int", [P, HB, C], i32)
        wd_int = sb("wd_int", [P, CB, HID], i32)
        wg_raw, wu_raw, wd_raw = sb("wg_raw", [P, HB, C]), sb("wu_raw", [P, HB, C]), sb("wd_raw", [P, CB, HID])
        ident = sb("ident", [P, P])
        even_head, odd_head = sb("even_head", [P, 1]), sb("odd_head", [P, 1])
        minus_half = sb("minus_half", [P, TT])
        low_sizes, low_scratch = sb("low_sizes", [P, 3]), sb("low_scratch", [P, CB, HID])
        ones_col = sb("ones_col", [P, 1])
        any_low = sb("any_low", [1, 1], i32)

        x_sb = [sb(f"x_sb{i}", [P, TT, C]) for i in range(2)]
        x_res = [sb(f"x_res{i}", [P, TT, C]) for i in range(2)]
        x2 = [sb(f"x2_{i}", [P, TT, C]) for i in range(2)]
        out_sb = [sb(f"out_sb{i}", [P, TT, C]) for i in range(2)]
        xn, x2n = sb("xn", [P, TT, C]), sb("x2n", [P, TT, C])
        xT_hi, xT_lo = sb("xT_hi", [P, CB, GT], f32r), sb("xT_lo", [P, CB, GT], f32r)
        x2T_hi, x2T_lo = sb("x2T_hi", [P, CB, GT], f32r), sb("x2T_lo", [P, CB, GT], f32r)
        yT_hi, yT_lo = sb("yT_hi", [P, CB, GT], f32r), sb("yT_lo", [P, CB, GT], f32r)
        qT = sb("qT", [P, CB, GT])
        kT = sb("kT", [P, CB, 2, GT])
        v_sb = sb("v_sb", [P, 2, 2, D, TT, PAIRS])
        v_stage = sb("v_stage", [P, 2, D, TT, PAIRS])
        probs = [sb(f"probs{t}", [P, HEADS * WIN]) for t in range(TT)]
        score_max = [sb(f"score_max{t}", [P, HEADS]) for t in range(TT)]
        pT = sb("pT", [P, 2 * TT, 4, P])
        prob_sum = [sb(f"prob_sum{t}", [P, HEADS]) for t in range(TT)]
        inv_sum = [sb(f"inv_sum{t}", [P, HEADS]) for t in range(TT)]
        attn_sb, ffn_sb = sb("attn_sb", [P, TT, C]), sb("ffn_sb", [P, TT, C])
        tanh_sb, gated, h_sb = (sb(n, [P, HP, 2 * GT]) for n in ("tanh_sb", "gated", "h_sb"))
        hT_hi, hT_lo = sb("hT_hi", [P, HP, 2, GT], f32r), sb("hT_lo", [P, HP, 2, GT], f32r)
        NORMS = ("in", "attn", "mid", "ffn")
        ACT_NORMS = ("in", "ffn")
        SCALE_STEPS = {n: 2 if n in ACT_NORMS else 1 for n in NORMS}
        stats = {n: sb(f"stats_{n}", [P, TT, 6]) for n in NORMS}
        mean_var = {n: sb(f"mean_var_{n}", [P, TT, 2]) for n in NORMS}
        neg_mean = {n: sb(f"neg_mean_{n}", [P, TT]) for n in ACT_NORMS}
        var_eps = {n: sb(f"var_eps_{n}", [P, TT]) for n in NORMS}
        rstd = {n: sb(f"rstd_{n}", [P, TT]) for n in NORMS}
        neg_mr = {n: sb(f"neg_mr_{n}", [P, TT]) for n in ACT_NORMS}

        score_ps = pb("score_ps", [P, 4, 512])
        turn0, turn1 = pb("turn0", [P, 512]), pb("turn1", [P, 512])
        pT_ps, yT_ps = pb("pT_ps", [P, 512]), pb("yT_ps", [P, CB, GT])

        w_loaded = [sem(f"w_loaded{i}") for i in range(5)]
        ident_set, masks_set, constants_set = sem("ident_set"), sem("masks_set"), sem("constants_set")
        gate_cast, up_down_cast = sem("gate_cast"), sem("up_down_cast")
        low_sized, low_summed, any_low_set = sem("low_sized"), sem("low_summed"), sem("any_low_set")
        wT_done, wT_hi_done, wT_lo_done = sem("wT_done"), sem("wT_hi_done"), sem("wT_lo_done")
        x_loaded = [sem(f"x_loaded{i}") for i in range(2)]
        x_kept = [sem(f"x_kept{i}") for i in range(2)]
        stored = [sem(f"stored{i}") for i in range(2)]
        norm_steps = {n: sem(f"norm_steps_{n}") for n in NORMS}
        norm_scales = {n: sem(f"norm_scales_{n}") for n in NORMS}
        normed = {n: sem(f"normed_{n}") for n in NORMS}
        xT_done, xT_hi_done, xT_lo_done = sem("xT_done"), sem("xT_hi_done"), sem("xT_lo_done")
        yT_hi_done, yT_lo_done = sem("yT_hi_done"), sem("yT_lo_done")
        x2T_done, x2T_hi_done, x2T_lo_done = sem("x2T_done"), sem("x2T_hi_done"), sem("x2T_lo_done")
        q_done, k_done, v_done = sem("q_done"), sem("k_done"), sem("v_done")
        q_out, k_even_out, k_odd_out = sem("q_out"), sem("k_even_out"), sem("k_odd_out")
        v_out, v_placed = sem("v_out"), sem("v_placed")
        scores_done = sem("scores_done")
        softmax_steps = sem("softmax_steps")
        exp_done = sem("exp_done")
        pT_done, pT_out, pv_done = sem("pT_done"), sem("pT_out"), sem("pv_done")
        probs_scaled = sem("probs_scaled")
        proj_done, attn_out, x2_done = sem("proj_done"), sem("attn_out"), sem("x2_done")
        gate_done, up_done = sem("gate_done"), sem("up_done")
        tanh_done, glu_steps = sem("tanh_done"), sem("glu_steps")
        h_hi_done, h_lo_done = sem("h_hi_done"), sem("h_lo_done")
        down_done, ffn_out, out_done = sem("down_done"), sem("ffn_out"), sem("out_done")

        class Group:

            def __init__(self, k, c):
                self.k, self.c = k, c
                self.number, self.parity, self.half = 2 * k + c, c % 2, k + c // 2
                self.live = not isinstance(k, int) or 0 <= 2 * k + c < NG

            def shift(self, by):
                return Group(self.k, self.c + by)

        def count(g, each, k):
            return g.number * each + k

        def nth(g, k=1):
            return (g.half + k) * 16

        def ahead(eng, *values):
            for v in values:
                if not isinstance(v, int):
                    eng.compute_val(v)

        LOOP_FROM, LOOP_TO = 4, NG - 4
        assert NG % 2 == 0

        FLAG_STEP = 0

        def first_steps(step):
            for s in range(-1, FLAG_STEP + 1):
                step(Group(0, s))

        def other_steps(eng, step):
            for s in range(FLAG_STEP + 1, LOOP_FROM):
                step(Group(0, s))
            with eng.Fori(LOOP_FROM // 2, LOOP_TO // 2) as k:
                step(Group(k, 0))
                step(Group(k, 1))
            for s in range(LOOP_TO, NG + 2):
                step(Group(0, s))

        def steps(eng, step):
            first_steps(step)
            other_steps(eng, step)

        def at_flag(s):
            return isinstance(s.k, int) and s.number == FLAG_STEP

        HALVES = (slice(0, WIN), slice(WIN, P))

        block = ctx.enter_context(nc.Block())

        def weight_turns():
            turns = []
            for raw, hi, lo, n in ((wa_raw, wa_hi, wa_lo, 3 * CB), (wp_raw, wp_hi, wp_lo, CB),
                                   (wg_raw, wg_hi, wg_lo, HB), (wu_raw, wu_hi, wu_lo, HB)):
                for r in range(0, n, 2):
                    blocks = [raw[:, r + i, c * P:(c + 1) * P] for c in range(CB) for i in range(2)]
                    turns.append((raw, blocks, hi[:, :, r * P:(r + 2) * P], lo[:, :, r * P:(r + 2) * P]))
            for b in range(0, HB, 2):
                blocks = [wd_raw[:, r, (b + i) * P:(b + i + 1) * P] for i in range(2) for r in range(CB)]
                turns.append((wd_raw, blocks, wd_hi[:, b:b + 2, :], wd_lo[:, b:b + 2, :]))
            return turns

        TURNS = weight_turns()
        W_BANKS = [turn0[:, :], turn1[:, :], pT_ps[:, :], yT_ps[:, :, :].rearrange("p a b -> p (a b)")]

        @block.sync
        def _(sp):
            def load(g):
                ahead(sp, g.number, nth(g, 0), count(g.shift(-2), 1, 1))
                if g.shift(-2).live:
                    sp.wait_ge(x_kept[g.parity], nth(g, 0))
                    sp.wait_ge(normed["in"], count(g.shift(-2), 1, 1))
                sp.dma_start(x_sb[g.parity][:, :, :], x_v[g.number, :, :, :]).then_inc(x_loaded[g.parity], 16)

            load(Group(0, 0))
            sp.dma_start(wa_raw[:, :, :], w_attn.rearrange("(r p) c -> p r c", p=P)).then_inc(w_loaded[0], 16)
            sp.dma_start(wp_raw[:, :, :], w_proj.rearrange("(r p) c -> p r c", p=P)).then_inc(w_loaded[1], 16)
            sp.dma_start(wg_int[:, :, :], w_gate.rearrange("(r p) c -> p r c", p=P)).then_inc(w_loaded[2], 16)
            sp.dma_start(wu_int[:, :, :], w_up.rearrange("(r p) c -> p r c", p=P)).then_inc(w_loaded[3], 16)
            sp.dma_start(wd_int[:, :, :], w_down.rearrange("(r p) c -> p r c", p=P)).then_inc(w_loaded[4], 16)

            load(Group(0, 1))

            def step(s):
                a, b, e = s.shift(1), s, s.shift(-2)
                if b.live:
                    ahead(sp, count(b, 1, 1))
                    sp.wait_ge(v_out, count(b, 1, 1))
                    for w, tokens in enumerate(HALVES):
                        for side, place in enumerate(HALVES):
                            sp.dma_start(v_sb[place, w, side, 0:D, :, :], v_stage[tokens, side, :, :, :])\
                              .then_inc(v_placed, 16)
                if a.live:
                    ahead(sp, nth(a), count(a.shift(-2), 1, 1))
                    sp.wait_ge(x_loaded[a.parity], nth(a))
                    if a.shift(-2).live:
                        sp.wait_ge(x2_done, count(a.shift(-2), 1, 1))
                    sp.dma_start(x_res[a.parity][:, :, :], x_sb[a.parity][:, :, :])\
                      .then_inc(x_kept[a.parity], 16)
                if e.live:
                    ahead(sp, e.number, count(e, 1, 1))
                    sp.wait_ge(out_done, count(e, 1, 1))
                    sp.dma_start(out_v[e.number, :, :, :], out_sb[e.parity][:, :, :])\
                      .then_inc(stored[e.parity], 16)
                if a.shift(2).live and a.live:
                    load(a.shift(2))

            steps(sp, step)
            for i in range(2):
                sp.wait_ge(stored[i], NG // 2 * 16)

        @block.gpsimd
        def _(pool):
            pool.memset(ident[:, :], 0.0).then_inc(ident_set, 1)
            pool.memset(minus_half[:, :], -0.5).then_inc(constants_set, 1)
            pool.wait_ge(ident_set, 1)
            pool.affine_select(out=ident[:, :], in_=ident[:, :], compare_op=ALU.not_equal, fill=1.0,
                               base=0, pattern=[[-1, P]], channel_multiplier=1).then_inc(ident_set, 1)
            pool.memset(v_sb[:, :, :, :, :, :], 0.0).then_inc(constants_set, 1)
            pool.memset(ones_col[:, :], 1.0).then_inc(constants_set, 1)

            def scales(norm, g):
                pool.wait_ge(norm_steps[norm], count(g, 3, 3))
                if g.shift(-1).live:
                    pool.wait_ge(normed[norm], count(g.shift(-1), 1, 1))
                pool.tensor_tensor(rstd[norm][:, :], var_eps[norm][:, :], minus_half[:, :], ALU.pow)\
                    .then_inc(norm_scales[norm], 1)
                if norm not in ACT_NORMS:
                    return
                pool.wait_ge(norm_scales[norm], count(g, 2, 1))
                pool.tensor_tensor(neg_mr[norm][:, :], neg_mean[norm][:, :], rstd[norm][:, :], ALU.mult)\
                    .then_inc(norm_scales[norm], 1)

            def scale_probs(g, t):
                p = probs[t][:, :].rearrange("p (b m e j) -> p m b e j", m=CB, e=2, j=WIN)
                inv = inv_sum[t][:, :].rearrange("p (b m e) -> p m b e", m=CB, e=2)
                pool.wait_ge(softmax_steps, count(g, 8, 4 * t + 4))
                for m in range(CB):
                    pool.tensor_tensor(p[:, m], p[:, m], inv[:, m].unsqueeze(3).broadcast_to([P, 4, 2, WIN]),
                                       ALU.mult).then_inc(probs_scaled, 1)

            def h_low(g, j):
                pool.wait_ge(h_hi_done, count(g, HP, j + 1))
                pool.tensor_tensor(hT_lo[:, j, :, :], h_sb[:, j, :].rearrange("p (b t) -> p b t", b=2),
                                   hT_hi[:, j, :, :].bitcast(f32), ALU.subtract).then_inc(h_lo_done, 1)

            def step(s):
                f, b, c, e = s.shift(2), s, s.shift(-1), s.shift(-2)
                if e.live:
                    h_low(e, 2)
                if c.live:
                    scales("attn", c)
                if b.live:
                    scale_probs(b, 0)
                if c.live:
                    scales("mid", c)
                if b.live:
                    scale_probs(b, 1)
                if e.live:
                    scales("ffn", e)
                if c.live:
                    h_low(c, 0)
                if f.live:
                    scales("in", f)
                if c.live:
                    h_low(c, 1)
                if e.live:
                    pool.wait_ge(normed["ffn"], count(e, 1, 1))
                    if e.shift(-2).live:
                        pool.wait_ge(stored[e.parity], nth(e, 0))
                    pool.tensor_tensor(out_sb[e.parity][:, :, :], ffn_sb[:, :, :], x2[e.parity][:, :, :],
                                       ALU.add).then_inc(out_done, 1)

            step(Group(0, -2))
            steps(pool, step)

        @block.tensor
        def _(pe):
            pe.wait_ge(ident_set, 2)
            for n, (raw, blocks, _, _) in enumerate(TURNS):
                if raw is wa_raw or raw is wp_raw:
                    pe.wait_ge(w_loaded[0 if raw is wa_raw else 1], 16)
                elif raw is wg_raw:
                    pe.wait_ge(gate_cast, 1)
                else:
                    pe.wait_ge(up_down_cast, 1 if raw is wu_raw else 2)
                if n >= len(W_BANKS):
                    pe.wait_ge(wT_lo_done, n + 1 - len(W_BANKS))
                bank = W_BANKS[n % len(W_BANKS)]
                for i, b in enumerate(blocks):
                    mm = pe.transpose(bank[:, i * P:(i + 1) * P], b, ident[:, :])
                mm.then_inc(wT_done, 1)
            pe.wait_ge(wT_lo_done, len(TURNS))
            pe.wait_ge(constants_set, 3)

            def turn_tokens(bank, src, done):
                for c in range(CB):
                    for t in range(TT):
                        mm = pe.transpose(bank[:, c * GT + t * P:c * GT + (t + 1) * P],
                                          src[:, t, c * P:(c + 1) * P], ident[:, :])
                mm.then_inc(done, 1)

            def split_product(out_ap, stationary, moving, blocks, skip=None):
                n = len(blocks)
                for i, blk in enumerate(blocks):
                    (s_hi, s_lo), (m_hi, m_lo) = stationary(blk), moving(blk)
                    products = [(s_hi, m_hi)]
                    if skip != "moving":
                        products.append((s_hi, m_lo))
                    if skip != "stationary":
                        products.append((s_lo, m_hi))
                    for k, (x, y) in enumerate(products):
                        mm = pe.matmul(out_ap, x, y, start=(i == 0 and k == 0),
                                       stop=(i == n - 1 and k == len(products) - 1))
                return mm

            def q_or_k(bank, first_block, done):
                for m in range(CB):
                    col = (first_block + m) * P
                    mm = split_product(bank[:, m * GT:(m + 1) * GT],
                                       lambda c: (wa_hi[:, c, col:col + P], wa_lo[:, c, col:col + P]),
                                       lambda c: (xT_hi[:, c, :], xT_lo[:, c, :]), range(CB))
                mm.then_inc(done, 1)

            def values():
                for t in range(TT):
                    mm = split_product(turn1[:, t * C:(t + 1) * C],
                                       lambda c: (xT_hi[:, c, t * P:(t + 1) * P], xT_lo[:, c, t * P:(t + 1) * P]),
                                       lambda c: (wa_hi[:, c, 2 * C:3 * C], wa_lo[:, c, 2 * C:3 * C]),
                                       range(CB))
                mm.then_inc(v_done, 1)

            def scores(t, m):
                for w in range(2):
                    at = t * P + w * WIN
                    for b in range(4):
                        mm = pe.matmul(score_ps[w * WIN:(w + 1) * WIN, b, m * P:(m + 1) * P],
                                       qT[32 * b:32 * b + 32, m, at:at + WIN],
                                       kT[32 * b:32 * b + 32, m, :, at:at + WIN],
                                       start=True, stop=True)
                if m == CB - 1:
                    mm.then_inc(scores_done, 1)

            def turn_probs(g, t, m):
                unit = 2 * t + m
                pe.wait_ge(probs_scaled, count(g, 4, unit + 1))
                if unit or g.shift(-1).live:
                    pe.wait_ge(pT_out, count(g, 4, unit))
                for b in range(4):
                    at = (2 * b + m) * P
                    mm = pe.transpose(pT_ps[:, b * P:(b + 1) * P], probs[t][:, at:at + P], ident[:, :])
                mm.then_inc(pT_done, 1)

            def weigh_values(g, t, m):
                unit = 2 * t + m
                pe.wait_ge(pT_out, count(g, 4, unit + 1))
                if unit == 0:
                    pe.wait_ge(v_placed, count(g, 64, 64))
                for w in range(2):
                    at = t * P + w * WIN
                    for b in range(4):
                        mm = pe.matmul(yT_ps[32 * b:32 * b + 32, m, at:at + WIN],
                                       v_sb[:, w, :, :, t, 4 * m + b].rearrange("p e d -> p (e d)"),
                                       pT[:, unit, b, w * WIN:(w + 1) * WIN], start=True, stop=True)
                mm.then_inc(pv_done, 1)

            def project():
                for t in range(TT):
                    mm = split_product(turn0[:, t * C:(t + 1) * C],
                                       lambda c: (yT_hi[:, c, t * P:(t + 1) * P], yT_lo[:, c, t * P:(t + 1) * P]),
                                       lambda c: (wp_hi[:, c, :], wp_lo[:, c, :]), range(CB))
                mm.then_inc(proj_done, 1)

            def hidden(bank, hi, lo, j, done, low):
                for i in range(2):
                    col = (2 * j + i) * P
                    mm = split_product(bank[:, i * GT:(i + 1) * GT],
                                       lambda c: (hi[:, c, col:col + P], lo[:, c, col:col + P]),
                                       lambda c: (x2T_hi[:, c, :], x2T_lo[:, c, :]), range(CB),
                                       skip=None if low else "stationary")
                mm.then_inc(done, 1)

            def down(low):
                for t in range(TT):
                    def h_of(x, k):
                        return x[:, k // 2, k % 2, t * P:(t + 1) * P]
                    mm = split_product(turn0[:, t * C:(t + 1) * C],
                                       lambda k: (h_of(hT_hi, k), h_of(hT_lo, k)),
                                       lambda k: (wd_hi[:, k, :], wd_lo[:, k, :]), range(HB),
                                       skip=None if low else "moving")
                mm.then_inc(down_done, 1)

            def sum_low_sizes():
                pe.wait_ge(low_sized, 3)
                pe.matmul(yT_ps[0:1, 0, 0:3], ones_col[:, :], low_sizes[:, :], start=True, stop=True)\
                  .then_inc(low_summed, 1)

            def step(s, low=True):
                a, b, c, e = s.shift(1), s, s.shift(-1), s.shift(-2)
                if b.live:
                    pe.wait_ge(q_out, count(b, 1, 1))
                    pe.wait_ge(k_even_out, count(b, 1, 1))
                    pe.wait_ge(k_odd_out, count(b, 1, 1))
                    if e.live:
                        pe.wait_ge(glu_steps, count(e, 2 * HP, 4))
                    elif c.live:
                        pe.wait_ge(softmax_steps, count(c, 8, 6))
                    scores(0, 0)
                    scores(0, 1)
                if c.live:
                    pe.wait_ge(yT_lo_done, count(c, 1, 1))
                    if e.live:
                        pe.wait_ge(glu_steps, count(e, 2 * HP, 5))
                    project()
                if at_flag(s):
                    sum_low_sizes()
                if b.live:
                    if e.live:
                        pe.wait_ge(glu_steps, count(e, 2 * HP, 6))
                    elif c.live:
                        pe.wait_ge(k_even_out, count(b, 1, 1))
                        pe.wait_ge(k_odd_out, count(b, 1, 1))
                    values()
                    pe.wait_ge(softmax_steps, count(b, 8, 2))
                    scores(1, 0)
                    scores(1, 1)
                if a.live:
                    pe.wait_ge(normed["in"], count(a, 1, 1))
                    if b.live:
                        pe.wait_ge(v_out, count(b, 1, 1))
                    turn_tokens(turn1, xn, xT_done)
                if e.live:
                    pe.wait_ge(h_lo_done, count(e, HP, HP))
                    if c.live:
                        pe.wait_ge(attn_out, count(c, 1, 1))
                    else:
                        pe.wait_ge(glu_steps, count(e, 2 * HP, 5))
                    down(low)
                if b.live:
                    turn_probs(b, 0, 0)
                if a.live:
                    pe.wait_ge(xT_lo_done, count(a, 1, 1))
                    q_or_k(turn1, 0, q_done)
                if b.live:
                    turn_probs(b, 0, 1)
                    if at_flag(s):
                        pe.wait_ge(any_low_set, 2)
                    weigh_values(b, 0, 0)
                if c.live:
                    pe.wait_ge(normed["mid"], count(c, 1, 1))
                    if e.live:
                        pe.wait_ge(ffn_out, count(e, 1, 1))
                    else:
                        pe.wait_ge(attn_out, count(c, 1, 1))
                    turn_tokens(turn0, x2n, x2T_done)
                if a.live:
                    pe.wait_ge(q_out, count(a, 1, 1))
                    q_or_k(turn1, CB, k_done)
                if b.live:
                    weigh_values(b, 0, 1)
                if c.live:
                    pe.wait_ge(x2T_lo_done, count(c, 1, 1))
                    if b.live:
                        pe.wait_ge(softmax_steps, count(b, 8, 6))
                    else:
                        pe.wait_ge(glu_steps, count(e, 2 * HP, 4))
                    hidden(score_ps[:, 0, :], wg_hi, wg_lo, 0, gate_done, low)
                    hidden(score_ps[:, 1, :], wu_hi, wu_lo, 0, up_done, low)
                    hidden(score_ps[:, 2, :], wg_hi, wg_lo, 1, gate_done, low)
                    hidden(score_ps[:, 3, :], wu_hi, wu_lo, 1, up_done, low)
                if b.live:
                    turn_probs(b, 1, 0)
                if c.live:
                    hidden(turn0[:, :], wg_hi, wg_lo, 2, gate_done, low)
                if b.live:
                    turn_probs(b, 1, 1)
                    weigh_values(b, 1, 0)
                if c.live:
                    if a.live:
                        pe.wait_ge(k_even_out, count(a, 1, 1))
                        pe.wait_ge(k_odd_out, count(a, 1, 1))
                    elif b.live:
                        pe.wait_ge(v_out, count(b, 1, 1))
                    else:
                        pe.wait_ge(glu_steps, count(e, 2 * HP, 6))
                    hidden(turn1[:, :], wu_hi, wu_lo, 2, up_done, low)
                if b.live:
                    weigh_values(b, 1, 1)

            first_steps(step)
            pe.wait_ge(any_low_set, 2)
            flag = pe.value_load(any_low[0:1, 0:1], min_val=0, max_val=1)
            with pe.If(flag > 0):
                other_steps(pe, lambda s: step(s, low=True))
            with pe.Else():
                other_steps(pe, lambda s: step(s, low=False))

        @block.scalar
        def _(act):
            def split(x):
                return x.rearrange("p (a b) -> p a b", a=2)

            def copy(to, of, done, scale=1.0):
                act.activation(to, of, ACT.Copy, scale=scale).then_inc(done, 1)

            def normalise(norm, g, to, of):
                act.wait_ge(norm_scales[norm], count(g, 2, 2))
                for t in range(TT):
                    last = act.activation(to[:, t, :], of[:, t, :], ACT.Identity,
                                          scale=rstd[norm][:, t:t + 1], bias=neg_mr[norm][:, t:t + 1])
                last.then_inc(normed[norm], 1)

            def values_out(g):
                act.wait_ge(v_done, count(g, 1, 1))
                copy(v_stage[:, :, :, :, :].rearrange("p e d t h -> p e d (t h)"),
                     turn1[:, :].rearrange("p (n e d) -> p e d n", e=2, d=D), v_out)

            def exponentials(g, t):
                act.wait_ge(softmax_steps, count(g, 8, 4 * t + 2))
                act.activation(probs[t][:, :], probs[t][:, :], ACT.Exp).then_inc(exp_done, 1)

            def probs_out(g, unit):
                act.wait_ge(pT_done, count(g, 4, unit + 1))
                copy(pT[:, unit, :, :], pT_ps[:, :].rearrange("p (b i) -> p b i", b=4), pT_out)

            def tanh(g, j, bank):
                act.wait_ge(gate_done, count(g, HP, j + 1))
                act.activation(tanh_sb[:, j, :], bank, ACT.Tanh, scale=0.5 * INT_SCALE).then_inc(tanh_done, 1)

            def h_high(g, j):
                act.wait_ge(glu_steps, count(g, 2 * HP, 2 * j + 2))
                if j == 0 and g.shift(-1).live:
                    act.wait_ge(down_done, count(g.shift(-1), 1, 1))
                copy(hT_hi[:, j, :, :], split(h_sb[:, j, :]), h_hi_done)

            def size_low_part(i):
                lo = (wg_lo, wu_lo, wd_lo)[i]
                act.wait_ge(wT_lo_done, len(TURNS))
                if i:
                    act.wait_ge(low_sized, i)
                scratch = low_scratch[:, :, :].rearrange("p a b -> p (a b)")\
                                               .rearrange("p (a b) -> p a b", a=lo.shape[1])
                act.activation(scratch, lo[:, :, :].bitcast(f32), ACT.Abs,
                               accum_out=low_sizes[:, i:i + 1]).then_inc(low_sized, 1)

            def step(s):
                a, b, c, e = s.shift(1), s, s.shift(-1), s.shift(-2)
                first = isinstance(s.k, int) and s.number == -1
                if c.live:
                    act.wait_ge(pv_done, count(c, 4, 4))
                    copy(yT_hi[:, :, :], yT_ps[:, :, :], yT_hi_done)
                if e.live:
                    h_high(e, 2)
                if a.live:
                    normalise("in", a, xn, x_sb[a.parity])
                if c.live:
                    act.wait_ge(proj_done, count(c, 1, 1))
                    if c.shift(-1).live:
                        act.wait_ge(x2_done, count(c.shift(-1), 1, 1))
                    copy(attn_sb[:, :, :], split(turn0[:, :]), attn_out)
                if b.live:
                    exponentials(b, 0)
                    values_out(b)
                if a.live:
                    act.wait_ge(xT_done, count(a, 1, 1))
                    copy(xT_hi[:, :, :], split(turn1[:, :]), xT_hi_done)
                if e.live:
                    act.wait_ge(down_done, count(e, 1, 1))
                    if e.shift(-1).live:
                        act.wait_ge(out_done, count(e.shift(-1), 1, 1))
                    copy(ffn_sb[:, :, :], split(turn0[:, :]), ffn_out)
                if b.live:
                    probs_out(b, 0)
                if first:
                    size_low_part(0)
                if a.live:
                    act.wait_ge(q_done, count(a, 1, 1))
                    copy(qT[:, :, :], split(turn1[:, :]), q_out, scale=Q_SCALE)
                if b.live:
                    probs_out(b, 1)
                if c.live:
                    act.wait_ge(x2T_done, count(c, 1, 1))
                    copy(x2T_hi[:, :, :], split(turn0[:, :]), x2T_hi_done)
                if b.live:
                    exponentials(b, 1)
                if first:
                    size_low_part(1)
                if a.live:
                    act.wait_ge(k_done, count(a, 1, 1))
                    copy(kT[:, :, 0, :], split(turn1[:, :]), k_even_out, scale=even_head[:, :])
                    copy(kT[:, :, 1, :], split(turn1[:, :]), k_odd_out, scale=odd_head[:, :])
                if first:
                    size_low_part(2)
                if c.live:
                    tanh(c, 0, score_ps[:, 0, :])
                    tanh(c, 1, score_ps[:, 2, :])
                if b.live:
                    probs_out(b, 2)
                if c.live:
                    h_high(c, 0)
                    tanh(c, 2, turn0[:, :])
                if b.live:
                    probs_out(b, 3)
                if e.live:
                    normalise("ffn", e, ffn_sb, ffn_sb)
                if c.live:
                    h_high(c, 1)

            for n, (raw, _, hi, _) in enumerate(TURNS):
                if raw is wg_raw and TURNS[n - 1][0] is not wg_raw:
                    act.wait_ge(w_loaded[2], 16)
                    copy(wg_raw[:, :, :], wg_int[:, :, :], gate_cast)
                act.wait_ge(wT_done, n + 1)
                copy(hi, split(W_BANKS[n % len(W_BANKS)]), wT_hi_done)
            act.wait_ge(masks_set, 2)
            steps(act, step)

        @block.vector
        def _(dve):
            def split(x):
                return x.rearrange("p (a b) -> p a b", a=2)

            dve.wait_ge(ident_set, 2)
            head_rows = ident[:, :].rearrange("p (a e d) -> p a e d", e=2, d=D)
            dve.tensor_reduce(even_head[:, :], head_rows[:, :, 0, :], AX.XY, ALU.add).then_inc(masks_set, 1)
            dve.tensor_reduce(odd_head[:, :], head_rows[:, :, 1, :], AX.XY, ALU.add).then_inc(masks_set, 1)

            def low(to, bank, hi, done):
                dve.tensor_tensor(to, bank, hi.bitcast(f32), ALU.subtract).then_inc(done, 1)

            def statistics(norm, g, x):
                for t in range(TT):
                    last = dve.bn_stats(stats[norm][:, t, :], x[:, t, :])
                last.then_inc(norm_steps[norm], 1)
                ahead(dve, count(g, 3, 1))
                dve.wait_ge(masks_set, 2)
                dve.wait_ge(norm_steps[norm], count(g, 3, 1))
                for t in range(TT):
                    last = dve.bn_aggr(mean_var[norm][:, t, :], stats[norm][:, t, :])
                last.then_inc(norm_steps[norm], 1)
                dve.wait_ge(norm_steps[norm], count(g, 3, 2))
                if g.shift(-1).live:
                    n = SCALE_STEPS[norm]
                    dve.wait_ge(norm_scales[norm], count(g.shift(-1), n, n))
                if norm in ACT_NORMS:
                    dve.tensor_scalar(neg_mean[norm][:, :], mean_var[norm][:, :, 0], -1.0, None, ALU.mult)
                dve.tensor_scalar(var_eps[norm][:, :], mean_var[norm][:, :, 1], LN_EPS, None,
                                  ALU.add).then_inc(norm_steps[norm], 1)

            def normalise(norm, g, to, of):
                dve.wait_ge(norm_scales[norm], count(g, 1, 1))
                for t in range(TT):
                    last = dve.tensor_scalar(to[:, t, :], of[:, t, :], mean_var[norm][:, t, 0:1],
                                             rstd[norm][:, t:t + 1], ALU.subtract, ALU.mult)
                last.then_inc(normed[norm], 1)

            def maximum(g, t):
                dve.wait_ge(scores_done, count(g, TT, t + 1))
                dve.tensor_reduce(score_max[t][:, :].rearrange("p (b h) -> p b h", b=4),
                                  score_ps[:, :, 0:4 * WIN].rearrange("p b (h j) -> p b h j", j=WIN),
                                  AX.X, ALU.max).then_inc(softmax_steps, 1)

            def less_maximum(g, t):
                dve.wait_ge(softmax_steps, count(g, 8, 4 * t + 1))
                dve.tensor_tensor(probs[t][:, :].rearrange("p (b h j) -> p b h j", b=4, j=WIN),
                                  score_ps[:, :, 0:4 * WIN].rearrange("p b (h j) -> p b h j", j=WIN),
                                  score_max[t][:, :].rearrange("p (b h) -> p b h", b=4).unsqueeze(3)
                                  .broadcast_to([P, 4, 4, WIN]), ALU.subtract).then_inc(softmax_steps, 1)

            def add_probs(g, t):
                dve.wait_ge(exp_done, count(g, TT, t + 1))
                dve.tensor_reduce(prob_sum[t][:, :], probs[t][:, :].rearrange("p (h j) -> p h j", j=WIN),
                                  AX.X, ALU.add).then_inc(softmax_steps, 1)

            def invert_sum(g, t):
                dve.wait_ge(softmax_steps, count(g, 8, 4 * t + 3))
                dve.reciprocal(inv_sum[t][:, :], prob_sum[t][:, :]).then_inc(softmax_steps, 1)

            def gate_out(g, j, g_bank):
                dve.wait_ge(tanh_done, count(g, HP, j + 1))
                dve.scalar_tensor_tensor(out=gated[:, j, :], in0=tanh_sb[:, j, :], scalar=1.0, in1=g_bank,
                                         op0=ALU.add, op1=ALU.mult).then_inc(glu_steps, 1)

            def times_up(g, j, u_bank):
                dve.wait_ge(glu_steps, count(g, 2 * HP, 2 * j + 1))
                dve.wait_ge(up_done, count(g, HP, j + 1))
                if g.shift(-1).live:
                    dve.wait_ge(h_lo_done, count(g.shift(-1), HP, j + 1))
                dve.scalar_tensor_tensor(out=h_sb[:, j, :], in0=u_bank, scalar=H_SCALE, in1=gated[:, j, :],
                                         op0=ALU.mult, op1=ALU.mult).then_inc(glu_steps, 1)

            def set_flag():
                dve.wait_ge(low_summed, 1)
                dve.tensor_scalar(low_sizes[0:1, :], yT_ps[0:1, 0, 0:3], 0.0, None,
                                  ALU.is_gt).then_inc(any_low_set, 1)
                dve.wait_ge(any_low_set, 1)
                dve.tensor_reduce(any_low[:, :], low_sizes[0:1, :], AX.X, ALU.max).then_inc(any_low_set, 1)

            def step(s):
                f, a, b, c, e = s.shift(2), s.shift(1), s, s.shift(-1), s.shift(-2)
                if c.live:
                    dve.wait_ge(yT_hi_done, count(c, 1, 1))
                    low(yT_lo[:, :, :], yT_ps[:, :, :], yT_hi[:, :, :], yT_lo_done)
                if e.live:
                    times_up(e, 2, turn1[:, :])
                if at_flag(s):
                    set_flag()
                if b.live:
                    maximum(b, 0)
                    less_maximum(b, 0)
                if c.live:
                    dve.wait_ge(attn_out, count(c, 1, 1))
                    statistics("attn", c, attn_sb)
                if b.live:
                    add_probs(b, 0)
                if c.live:
                    normalise("attn", c, attn_sb, attn_sb)
                if b.live:
                    invert_sum(b, 0)
                if c.live:
                    dve.wait_ge(normed["attn"], count(c, 1, 1))
                    dve.wait_ge(x_kept[c.parity], nth(c))
                    if c.shift(-2).live:
                        dve.wait_ge(out_done, count(c.shift(-2), 1, 1))
                    dve.tensor_tensor(x2[c.parity][:, :, :], attn_sb[:, :, :], x_res[c.parity][:, :, :],
                                      ALU.add).then_inc(x2_done, 1)
                if a.live:
                    dve.wait_ge(xT_hi_done, count(a, 1, 1))
                    low(xT_lo[:, :, :], split(turn1[:, :]), xT_hi[:, :, :], xT_lo_done)
                if c.live:
                    dve.wait_ge(x2_done, count(c, 1, 1))
                    statistics("mid", c, x2[c.parity])
                if b.live:
                    maximum(b, 1)
                if c.live:
                    normalise("mid", c, x2n, x2[c.parity])
                if b.live:
                    less_maximum(b, 1)
                if c.live:
                    dve.wait_ge(x2T_hi_done, count(c, 1, 1))
                    low(x2T_lo[:, :, :], split(turn0[:, :]), x2T_hi[:, :, :], x2T_lo_done)
                if b.live:
                    add_probs(b, 1)
                    invert_sum(b, 1)
                if e.live:
                    dve.wait_ge(ffn_out, count(e, 1, 1))
                    statistics("ffn", e, ffn_sb)
                if c.live:
                    gate_out(c, 0, score_ps[:, 0, :])
                    times_up(c, 0, score_ps[:, 1, :])
                    gate_out(c, 1, score_ps[:, 2, :])
                    times_up(c, 1, score_ps[:, 3, :])
                if f.live:
                    dve.wait_ge(x_loaded[f.parity], nth(f))
                    statistics("in", f, x_sb[f.parity])
                if c.live:
                    gate_out(c, 2, turn0[:, :])

            step(Group(0, -2))
            for n, (raw, _, hi, lo) in enumerate(TURNS):
                if raw is wg_raw and TURNS[n - 1][0] is not wg_raw:
                    for i, (to, of) in enumerate(((wu_raw, wu_int), (wd_raw, wd_int))):
                        dve.wait_ge(w_loaded[3 + i], 16)
                        dve.tensor_copy(to[:, :, :], of[:, :, :]).then_inc(up_down_cast, 1)
                dve.wait_ge(wT_hi_done, n + 1)
                low(lo, split(W_BANKS[n % len(W_BANKS)]), hi, wT_lo_done)
            steps(dve, step)


_INS = ["L0_attn_x", "L0_attn_w_attn", "L0_attn_w_proj", "L0_ffn_w_gate", "L0_ffn_w_up", "L0_ffn_w_down"]


def kernel(**inputs):
    import numpy as _np
    import concourse.bacc as _bacc
    from concourse import mybir as _mybir
    from concourse.bass_utils import run_bass_kernel_spmd as _run

    nc = _bacc.Bacc("TRN2", target_bir_lowering=False, num_devices=1)
    arrays, args = {}, []
    for name in _INS:
        a = _np.ascontiguousarray(inputs[name])
        arrays[f"in_{name}_dram"] = a
        args.append(nc.dram_tensor(f"in_{name}_dram", a.shape, _mybir.dt.from_np(a.dtype), kind="ExternalInput").ap())
    out = nc.dram_tensor("out_dram", inputs["L0_attn_x"].shape, _mybir.dt.float32, kind="ExternalOutput").ap()
    sandwich_block(nc, *args, out)
    return _run(nc, [arrays], core_ids=[0]).results[0]["out_dram"]
```
